# Optimizing a Trainium2 kernel written in Bass

```python
import numpy as np
import jax
import jax.numpy as jnp

def _softmax(x, axis=-1):
    return jax.nn.softmax(x, axis=axis)

def _gelu(x):
    return jax.nn.gelu(x, approximate=True)

def _silu(x):
    return jax.nn.silu(x)

def _sigmoid(x):
    return jax.nn.sigmoid(x)

def _layernorm(x, axis=-1, eps=1e-05):
    m = jnp.mean(x, axis=axis, keepdims=True)
    v = jnp.var(x, axis=axis, keepdims=True)
    return (x - m) / jnp.sqrt(v + eps)

def _scatter_add(tgt, idx, src, axis=0):
    return tgt.at[idx].add(src)

def _segment_sum(src, seg, n):
    return jax.ops.segment_sum(src, seg, n)
kernel_name = 'mk_adaln_ffn_d1_seqx_r4_040c91'

def setup_inputs(seed: int=0):
    np.random.seed(seed)
    _w = jnp.asarray

    def _rec_inputs():
        import jax
        import jax.numpy as jnp
        _rk = jax.random.key(seed)
        x = 8.748e-05 + 1 * jax.random.normal(jax.random.fold_in(_rk, 1), (8, 256, 512), jnp.float32)
        _lenS = 256 - jax.random.randint(jax.random.fold_in(_rk, 7), (8,), 0, max(1, 256 // 4) + 1, jnp.int32)
        _lenS2 = 256 - jax.random.randint(jax.random.fold_in(_rk, 8), (8,), 0, max(1, 256 // 4) + 1, jnp.int32)
        cond_2048 = -9.80646e-05 + 1.00041 * jax.random.normal(jax.random.fold_in(_rk, 11), (8, 512), jnp.float32)
        return (x, cond_2048)
    x, cond_2048 = _rec_inputs()

    def _L0_cond_setup():
        import jax, jax.numpy as jnp
        import numpy as np
        DT = 0.01
        EPSILON = 0.08
        ALPHA = 0.7
        BETA = 0.8
        CLAMP = 20.0
        B, T, N = (64, 128, 512)

        def _derivative(q, p, drive, coupling, bias):
            i_couple = jnp.tanh(q) @ coupling.T
            dq = q - q ** 3 / 3.0 - p + drive + i_couple + bias
            dp = EPSILON * (q + ALPHA - BETA * p)
            return (dq, dp)

        def _rk4_step(q, p, drive, coupling, bias):
            dq1, dp1 = _derivative(q, p, drive, coupling, bias)
            dq2, dp2 = _derivative(q + 0.5 * DT * dq1, p + 0.5 * DT * dp1, drive, coupling, bias)
            dq3, dp3 = _derivative(q + 0.5 * DT * dq2, p + 0.5 * DT * dp2, drive, coupling, bias)
            dq4, dp4 = _derivative(q + DT * dq3, p + DT * dp3, drive, coupling, bias)
            q_next = q + DT / 6.0 * (dq1 + 2 * dq2 + 2 * dq3 + dq4)
            p_next = p + DT / 6.0 * (dp1 + 2 * dp2 + 2 * dp3 + dp4)
            q_next = jnp.clip(q_next, -CLAMP, CLAMP)
            p_next = jnp.clip(p_next, -CLAMP, CLAMP)
            return (q_next, p_next)
        key = jax.random.key(seed)
        k1, k2, k3, k4 = jax.random.split(key, 4)
        return {'q0': jax.random.normal(k1, (B, N), dtype=jnp.float32), 'p0': jax.random.normal(k2, (B, N), dtype=jnp.float32), 'input_drive_seq': jax.random.normal(k3, (B, T, N), dtype=jnp.float32), 'coupling': jax.random.normal(k4, (N, N), dtype=jnp.float32) * 0.01, 'bias': jnp.zeros((N,), dtype=jnp.float32)}
    _L0_cond_all = _L0_cond_setup()
    _L0_cond_in = {k: v for k, v in _L0_cond_all.items() if k in ('coupling', 'bias')}
    del _L0_cond_all

    def _L0_ffn_setup():
        import jax, jax.numpy as jnp
        import numpy as np
        HIDDEN = 512
        INTER = 2048
        SCALE = 64.0

        def fwht(x):
            orig_shape = x.shape
            n = orig_shape[-1]
            x = x.reshape(-1, n)
            h = 1
            while h < n:
                x = x.reshape(-1, n // (2 * h), 2, h)
                a, b = (x[:, :, 0, :], x[:, :, 1, :])
                x = jnp.stack([a + b, a - b], axis=2).reshape(-1, n)
                h *= 2
            return (x / jnp.sqrt(jnp.asarray(n, x.dtype))).reshape(orig_shape)
        key = jax.random.key(seed)
        ks = jax.random.split(key, 8)
        inp = jax.random.normal(ks[0], (4, 512, HIDDEN), dtype=jnp.float32)
        SU_ug = jnp.where(jax.random.bernoulli(ks[1], 0.5, (HIDDEN,)), 1.0, -1.0).astype(jnp.float32)
        SU_dp = jnp.where(jax.random.bernoulli(ks[2], 0.5, (INTER,)), 1.0, -1.0).astype(jnp.float32)
        Wscale_ug = jax.random.uniform(ks[3], (2 * INTER,), jnp.float32, 0.5, 1.5)
        Wscale_dp = jax.random.uniform(ks[4], (HIDDEN,), jnp.float32, 0.5, 1.5)
        W_up = jax.random.normal(ks[5], (INTER, HIDDEN), dtype=jnp.float32) * 0.02
        W_gate = jax.random.normal(ks[6], (INTER, HIDDEN), dtype=jnp.float32) * 0.02
        W_down = jax.random.normal(ks[7], (HIDDEN, INTER), dtype=jnp.float32) * 0.02
        return {'input': inp, 'SU_ug': SU_ug, 'SU_dp': SU_dp, 'Wscale_ug': Wscale_ug, 'Wscale_dp': Wscale_dp, 'W_up': W_up, 'W_gate': W_gate, 'W_down': W_down}
    _L0_ffn_all = _L0_ffn_setup()
    _L0_ffn_in = {k: v for k, v in _L0_ffn_all.items() if k in ('SU_ug', 'SU_dp', 'Wscale_ug', 'Wscale_dp', 'W_up', 'W_gate', 'W_down')}
    del _L0_ffn_all
    return {'x': x, 'cond_2048': cond_2048, 'L0_cond_coupling': _L0_cond_in['coupling'], 'L0_cond_bias': _L0_cond_in['bias'], 'L0_ffn_SU_ug': _L0_ffn_in['SU_ug'], 'L0_ffn_SU_dp': _L0_ffn_in['SU_dp'], 'L0_ffn_Wscale_ug': _L0_ffn_in['Wscale_ug'], 'L0_ffn_Wscale_dp': _L0_ffn_in['Wscale_dp'], 'L0_ffn_W_up': _L0_ffn_in['W_up'], 'L0_ffn_W_gate': _L0_ffn_in['W_gate'], 'L0_ffn_W_down': _L0_ffn_in['W_down']}

def reference(x, cond_2048, L0_cond_coupling, L0_cond_bias, L0_ffn_SU_ug, L0_ffn_SU_dp, L0_ffn_Wscale_ug, L0_ffn_Wscale_dp, L0_ffn_W_up, L0_ffn_W_gate, L0_ffn_W_down):
    import jax
    import jax.numpy as jnp

    def _L0_cond_ref(q0, p0, input_drive_seq, coupling, bias):
        import jax, jax.numpy as jnp
        import numpy as np
        DT = 0.01
        EPSILON = 0.08
        ALPHA = 0.7
        BETA = 0.8
        CLAMP = 20.0
        B, T, N = (64, 128, 512)

        def _derivative(q, p, drive, coupling, bias):
            i_couple = jnp.tanh(q) @ coupling.T
            dq = q - q ** 3 / 3.0 - p + drive + i_couple + bias
            dp = EPSILON * (q + ALPHA - BETA * p)
            return (dq, dp)

        def _rk4_step(q, p, drive, coupling, bias):
            dq1, dp1 = _derivative(q, p, drive, coupling, bias)
            dq2, dp2 = _derivative(q + 0.5 * DT * dq1, p + 0.5 * DT * dp1, drive, coupling, bias)
            dq3, dp3 = _derivative(q + 0.5 * DT * dq2, p + 0.5 * DT * dp2, drive, coupling, bias)
            dq4, dp4 = _derivative(q + DT * dq3, p + DT * dp3, drive, coupling, bias)
            q_next = q + DT / 6.0 * (dq1 + 2 * dq2 + 2 * dq3 + dq4)
            p_next = p + DT / 6.0 * (dp1 + 2 * dp2 + 2 * dp3 + dp4)
            q_next = jnp.clip(q_next, -CLAMP, CLAMP)
            p_next = jnp.clip(p_next, -CLAMP, CLAMP)
            return (q_next, p_next)
        drive_tbn = jnp.swapaxes(input_drive_seq, 0, 1)

        def scan_fn(carry, drive):
            q, p = carry
            q, p = _rk4_step(q, p, drive, coupling, bias)
            return ((q, p), q)
        (_, _), q_trace_tbn = jax.lax.scan(scan_fn, (q0, p0), drive_tbn)
        return jnp.swapaxes(q_trace_tbn, 0, 1)

    def _L0_ffn_ref(input, SU_ug, SU_dp, Wscale_ug, Wscale_dp, W_up, W_gate, W_down):
        import jax, jax.numpy as jnp
        import numpy as np
        HIDDEN = 512
        INTER = 2048
        SCALE = 64.0

        def fwht(x):
            orig_shape = x.shape
            n = orig_shape[-1]
            x = x.reshape(-1, n)
            h = 1
            while h < n:
                x = x.reshape(-1, n // (2 * h), 2, h)
                a, b = (x[:, :, 0, :], x[:, :, 1, :])
                x = jnp.stack([a + b, a - b], axis=2).reshape(-1, n)
                h *= 2
            return (x / jnp.sqrt(jnp.asarray(n, x.dtype))).reshape(orig_shape)
        n = SU_ug.shape[0]
        x = input.reshape(-1, n)
        x = fwht(x * SU_ug) / SCALE
        x_up = x @ W_up.T * (Wscale_ug[:INTER] * SCALE)
        x_gate = x @ W_gate.T * (Wscale_ug[INTER:] * SCALE)
        x = jax.nn.silu(x_gate) * x_up
        x = fwht(x * SU_dp) / SCALE
        x = x @ W_down.T * (Wscale_dp * SCALE)
        return x.reshape(input.shape)
    x = x + _L0_ffn_ref(_L0_cond_ref(cond_2048, cond_2048, x, L0_cond_coupling, L0_cond_bias), L0_ffn_SU_ug, L0_ffn_SU_dp, L0_ffn_Wscale_ug, L0_ffn_Wscale_dp, L0_ffn_W_up, L0_ffn_W_gate, L0_ffn_W_down)
    return x

_drawn_inputs = setup_inputs


def setup_inputs(seed=0):
    import zlib

    import numpy as np

    out = dict(_drawn_inputs(seed))
    spreads = {'L0_cond_bias': (0.0, 0.1)}
    factors = {}
    for name, (base, spread) in spreads.items():
        noise = np.random.default_rng([zlib.crc32(name.encode()), seed]).standard_normal(out[name].shape)
        drawn = base * np.exp(spread * noise) if base else spread * noise
        out[name] = jnp.asarray(drawn.astype(out[name].dtype))
    for name, factor in factors.items():
        out[name] = (out[name] * factor).astype(out[name].dtype)
    return out
```

```python
from contextlib import ExitStack

import numpy as np

import concourse.bass as bass
from concourse import mybir

F32 = mybir.dt.float32
F16 = mybir.dt.float16
BF16 = mybir.dt.bfloat16
ALU = mybir.AluOpType
ACT = mybir.ActivationFunctionType
AX = mybir.AxisListType

P = 128
B = 8
T = 256
N = 512
INTER = 2048
KT = N // P
IT = INTER // P
SW = KT * B

DT = 0.01
EPSILON = 0.08
ALPHA = 0.7
BETA = 0.8
CLAMP = 20.0
S = 64.0
A = [DT / 2, DT / 2, DT, DT / 6]
P_SHIFT = ALPHA / BETA
_E, _Z = EPSILON * DT, EPSILON * BETA * DT
P_SELF = -_Z + _Z ** 2 / 2 - _Z ** 3 / 6 + _Z ** 4 / 24
P_FROM = [_E / 6 * (1 - _Z + _Z ** 2 / 2 - _Z ** 3 / 4), _E / 6 * (2 - _Z + _Z ** 2 / 2),
          _E / 6 * (2 - _Z), _E / 6]
AQ = [A[3], A[0], A[1], A[2]]

BODY_STEPS = 2
SLOTS = 4 * BODY_STEPS
ROWS = 256
RT = ROWS // P
CHUNK_STEPS = ROWS // B
CHUNKS = T // CHUNK_STEPS
BODIES = CHUNK_STEPS // BODY_STEPS
assert BODIES == IT
FP16_TOP = 1024.0

V_BIAS, V_SUUG, V_WUP, V_WGATE, V_SUDP, V_COLS = 0, 4, 8, 24, 40, 56


def build(nc, x_state, x_rows, cond, coupling, w_up, w_gate, w_down, vectors, ws_down, hadamard,
          identity, out):
    with ExitStack() as ctx:
        def sb(name, shape, dt=F32):
            return ctx.enter_context(nc.sbuf_tensor(name, shape, dt))

        def sem(name):
            return ctx.enter_context(nc.semaphore(name))

        raw = sb("raw", [P, IT * N])
        c_raw = raw[:, 0:KT * N]
        c_hi = sb("c_hi", [P, KT, N], F16)
        c_lo = sb("c_lo", [P, KT, N], F16)
        wu_hi = sb("wu_hi", [P, KT * INTER], F16)
        wu_lo = sb("wu_lo", [P, KT * INTER], F16)
        wg_hi = sb("wg_hi", [P, KT * INTER], F16)
        wg_lo = sb("wg_lo", [P, KT * INTER], F16)
        wd_buf = sb("wd_buf", [P, IT * N])
        wd_parts = wd_buf[:, :].bitcast(F16)
        wd_hi = wd_parts[:, 0:IT * N]
        wd_lo = wd_parts[:, IT * N:2 * IT * N]
        vec = sb("vec", [P, V_COLS])
        h128 = sb("h128", [P, P])
        ident = sb("ident", [P, P])
        ones = sb("ones", [1, P])
        wsd_row = sb("wsd_row", [1, N])
        wsd_all = sb("wsd_all", [P, N])
        had_p = sb("had_p", [P, KT, P], F16)
        had_m = sb("had_m", [P, KT, P], F16)
        peak = sb("peak", [P, 2])
        top = sb("top", [1, 4])
        unscale = sb("unscale", [P, 2])
        wscale = sb("wscale", [P, 2])
        dpeak = sb("dpeak", [P, IT])
        dunscale = sb("dunscale", [P, IT])
        dscale = sb("dscale", [P, IT])
        gscale = sb("gscale", [P, IT])
        uscale = sb("uscale", [P, IT])
        utmp = sb("utmp", [P, 2, IT])
        warm = sb("warm", [P, 1])
        bias = sb("bias", [P, KT])

        drive = sb("drive", [P, (T + 1) * SW])
        q_parts = drive[:, :].bitcast(F16)
        t_parts = sb("t_parts", [P, KT, 2, B], F16)
        t_full = sb("t_full", [P, SW])
        r = sb("r", [P, 4, SW])
        q = sb("q", [P, SW])
        q_raw = sb("q_raw", [P, SW])
        q_sq = sb("q_sq", [P, 4, SW])
        fq = sb("fq", [P, 4, SW])
        kq = sb("kq", [P, 4, SW])
        ksum = sb("ksum", [P, SW])
        ksum_push = sb("ksum_push", [P, SW])
        push_last = sb("push_last", [P, SW])
        r_clip = sb("r_clip", [P, SW])
        p = sb("p", [P, SW])
        p_raw = sb("p_raw", [P, SW])
        p_weight = sb("p_weight", [P, 4, SW])
        p_part = sb("p_part", [P, 5, SW])
        p_acc = sb("p_acc", [P, 4, SW])
        push = sb("push", [P, 4, SW])
        push_old = sb("push_old", [P, 3, SW])
        push_base = sb("push_base", [P, 2, SW])

        xf = sb("xf", [P, 2, ROWS])
        xh_hi = sb("xh_hi", [P, 2, KT * ROWS], F16)
        xh_lo = sb("xh_lo", [P, 2, KT * ROWS], F16)
        xh_hi_f = xh_hi[:, :, :].rearrange("p a b -> p (a b)")
        xh_lo_f = xh_lo[:, :, :].rearrange("p a b -> p (a b)")
        sil = sb("sil", [P, ROWS])
        up = sb("up", [P, ROWS])
        hid = sb("hid", [P, ROWS])
        hid_hi = sb("hid_hi", [P, ROWS], BF16)
        hid_lo = sb("hid_lo", [P, ROWS], BF16)
        x_res = sb("x_res", [P, RT, N])
        y_sb = sb("y_sb", [P, RT, N])

        rec = ctx.enter_context(nc.psum_tensor("rec", [P, 3 * 512], F32))
        PART = 256
        prod = rec[:, 512:1024].rearrange("p (s c) -> p s c", s=2)
        sum_full = rec[:, 512:1280].rearrange("p (s c) -> p c s", s=3)[:, 0:SW, :]
        sum_small = rec[:, 256:1024].rearrange("p (s c) -> p c s", s=3)[:, 0:SW, :]
        b_small = rec[:, PART:PART + SW]
        b_full = rec[:, 1024:1024 + SW]
        ps_gate, ps_up, ps_had, ps_y0, ps_y1 = [
            ctx.enter_context(nc.psum_tensor(n, [P, 512], F32))
            for n in ("ps_gate", "ps_up", "ps_had", "ps_y0", "ps_y1")]
        ps_y = [ps_y0, ps_y1]

        vec_in, had_in, ident_in, cond_in, drive_in, wsd_in = [
            sem(n) for n in ("vec_in", "had_in", "ident_in", "cond_in", "drive_in", "wsd_in")]
        raw_in, raw_free, peaks_found, peaks_turned, top_found, top_spread, scale_set, \
            unscale_set, w_hi_split, w_lo_split = [
                sem(n) for n in ("raw_in", "raw_free", "peaks_found", "peaks_turned", "top_found",
                                 "top_spread", "scale_set", "unscale_set", "w_hi_split",
                                 "w_lo_split")]
        fly_add, fly_sub, wd_rotated, wd_copied, d_unscale_set, d_scale_set, wd_hi_split, \
            wd_lo_split = [
                sem(n) for n in ("fly_add", "fly_sub", "wd_rotated", "wd_copied", "d_unscale_set",
                                 "d_scale_set", "wd_hi_split", "wd_lo_split")]
        c_hi_split, c_lo_split, ones_set, wsd_spread, wsd_set, had_set, drive_set, scales_step, \
            table_warm, bias_set, weight_set = [
                sem(n) for n in ("c_hi_split", "c_lo_split", "ones_set", "wsd_spread", "wsd_set",
                                 "had_set", "drive_set", "scales_step", "table_warm",
                                 "bias_set", "weight_set")]
        r_ready, thi_ready, tfull_ready, tlo_ready, prod_ready, kq_ready, sq_ready, fq_ready, \
            bfull_ready, bsmall_ready = [
                sem(n) for n in ("r_ready", "thi_ready", "tfull_ready", "tlo_ready", "prod_ready",
                                 "kq_ready", "sq_ready", "fq_ready", "bfull_ready",
                                 "bsmall_ready")]
        rclip_ready, push0_ready, ksum_ready, ksump_ready, last_ready, qraw_ready, q_ready, \
            praw_ready, p_ready, qhi_ready, qlo_ready = [
                sem(n) for n in ("rclip_ready", "push0_ready", "ksum_ready", "ksump_ready",
                                 "last_ready", "qraw_ready", "q_ready", "praw_ready", "p_ready",
                                 "qhi_ready", "qlo_ready")]
        base_ready, old_ready, push_ready, ppart_ready, pacc_ready = [
            sem(n) for n in ("base_ready", "old_ready", "push_ready", "ppart_ready",
                             "pacc_ready")]
        had_done, xf_ready, xhi_ready, xlo_ready, y_copied, y_scaled, y_ready, x_in, out_done = [
            sem(n) for n in ("had_done", "xf_ready", "xhi_ready", "xlo_ready", "y_copied",
                             "y_scaled", "y_ready", "x_in", "out_done")]
        gate_done, up_done, sil_ready, up_ready, hid_ready, hidhi_ready, hidlo_ready, down_done = [
            sem(n) for n in ("gate_done", "up_done", "sil_ready", "up_ready", "hid_ready",
                             "hidhi_ready", "hidlo_ready", "down_done")]

        block = ctx.enter_context(nc.Block())

        def run_bodies(eng, body, idle=None):
            def chunk(c, recur):
                one = isinstance(c, int) and c == 1
                body(c, 0, c * BODIES, recur, True, not one, not one)
                body(c, 1, c * BODIES + 1, recur, False, True, not one)
                body(c, 2, c * BODIES + 2, recur, False, True, True)
                with eng.Fori(3, BODIES) as j:
                    body(c, j, c * BODIES + j, recur, False, True, True)

            with eng.Fori(0, BODIES) as n:
                body(0, None, n, True, False, False, False)
            chunk(1, True)
            with eng.Fori(2, CHUNKS) as c:
                chunk(c, True)
            if idle:
                idle()
            chunk(CHUNKS, False)
            c = CHUNKS + 1
            body(c, 0, c * BODIES, False, False, True, True)
            body(c, 1, c * BODIES + 1, False, False, False, True)
            body(c, 2, c * BODIES + 2, False, False, False, False)

        @block.sync
        def _(sp):
            sp.dma_start(vec[:, :], vectors).then_inc(vec_in, 16)
            sp.dma_start(q[:, :], cond).then_inc(cond_in, 16)
            sp.dma_start(c_raw.rearrange("p (k n) -> p k n", k=KT),
                         coupling.rearrange("(k p) n -> p k n", p=P)).then_inc(raw_in, 16)
            sp.dma_start(drive[:, 0:T * SW], x_state).then_inc(drive_in, 16)
            sp.dma_start(h128[:, :], hadamard).then_inc(had_in, 16)
            sp.dma_start(ident[:, :], identity).then_inc(ident_in, 16)
            sp.dma_start(wsd_row[:, :], ws_down).then_inc(wsd_in, 16)
            for i, w in enumerate((w_up, w_gate)):
                sp.wait_ge(raw_free, i + 1)
                sp.dma_start(raw[:, :].rearrange("p (k n) -> p k n", k=KT),
                             w.rearrange("(k p) n -> p k n", p=P)).then_inc(raw_in, 16)
            sp.wait_ge(raw_free, 3)
            sp.dma_start(raw[:, :].rearrange("p (k n) -> p k n", k=IT),
                         w_down.rearrange("(k p) n -> p k n", p=P)).then_inc(raw_in, 16)

            def chunk_io(h, first):
                if not first:
                    sp.wait_ge(out_done, 16 * h)
                sp.dma_start(x_res[:, :, :],
                             x_rows[bass.ds(h * RT * P, RT * P), :].rearrange("(a p) n -> p a n", p=P)
                             ).then_inc(x_in, 16)
                sp.wait_ge(y_ready, RT * h + RT)
                sp.dma_start(out[bass.ds(h * RT * P, RT * P), :].rearrange("(a p) n -> p a n", p=P),
                             y_sb[:, :, :]).then_inc(out_done, 16)

            chunk_io(0, True)
            with sp.Fori(1, CHUNKS) as h:
                chunk_io(h, False)
            sp.wait_ge(out_done, 16 * CHUNKS)

        @block.scalar
        def _(act):
            act.wait_ge(ones_set, 2)
            act.activation(warm[:, :], warm[:, :], ACT.Silu).then_inc(table_warm, 1)
            for i, hi in enumerate((wu_hi, wg_hi)):
                act.wait_ge(scale_set, i + 1)
                act.activation(hi[:, :], raw[:, :], ACT.Identity,
                               scale=wscale[:, i:i + 1]).then_inc(w_hi_split, 1)
            for i in range(IT):
                act.wait_ge(wd_rotated, i + 1)
                act.activation(raw[:, i * N:(i + 1) * N], [ps_gate, ps_up][i % 2][:, :],
                               ACT.Copy).then_inc(wd_copied, 1)
            act.wait_ge(d_scale_set, 1)
            for i in range(IT):
                act.activation(wd_hi[:, i * N:(i + 1) * N], raw[:, i * N:(i + 1) * N], ACT.Identity,
                               scale=dscale[:, i:i + 1]).then_inc(wd_hi_split, 1)
            act.wait_ge(wsd_spread, 1)
            act.activation(wsd_all[:, :], ps_had[:, :], ACT.Copy).then_inc(wsd_set, 1)

            def stage(n, s):
                i = s % 4
                g = n * SLOTS + s
                act.wait_ge(r_ready, g + 1)
                act.activation(t_parts[:, :, 0, :], r[:, i, :].rearrange("p (k b) -> p k b", k=KT),
                               ACT.Tanh, scale=AQ[i] / S).then_inc(thi_ready, 1)
                act.activation(t_full[:, :], r[:, i, :], ACT.Tanh,
                               scale=AQ[i] / S).then_inc(tfull_ready, 1)

            def ffn(c, j, n, s, had, gate, down):
                if down and s == 0:
                    act.wait_ge(up_done, n - 17)
                    act.wait_ge(hid_ready, n - 18)
                    act.activation(up[:, :], ps_up[:, 0:ROWS], ACT.Identity,
                                   scale=uscale[:, bass.ds((n - 18) % IT, 1)]).then_inc(up_ready, 1)
                if down and s == 1:
                    act.wait_ge(hid_ready, n - 17)
                    act.wait_ge(down_done, n - 18)
                    act.activation(hid_hi[:, :], hid[:, :], ACT.Copy).then_inc(hidhi_ready, 1)
                if gate and s == 4:
                    act.wait_ge(gate_done, n - 16)
                    act.wait_ge(hid_ready, n - 17)
                    act.activation(sil[:, :], ps_gate[:, 0:ROWS], ACT.Silu,
                                   scale=gscale[:, bass.ds((n - 17) % IT, 1)]).then_inc(sil_ready, 1)
                if had and s in (3, 6):
                    half = s // 4
                    act.wait_ge(had_done, 2 * (c - 1) + half + 1)
                    act.wait_ge(xlo_ready, KT * (c - 1) + 2 * half)
                    for i in range(2):
                        act.activation(xf[:, i, :], ps_had[:, i * ROWS:(i + 1) * ROWS],
                                       ACT.Copy).then_inc(xf_ready, 1)
                if isinstance(j, int) and j == 2 and s in (0, 2) and not (isinstance(c, int) and c == 1):
                    a = s // 2
                    act.wait_ge(down_done, (c - 1) * BODIES)
                    act.wait_ge(x_in, 16 * (c - 1))
                    act.activation(y_sb[:, a, :], ps_y[a][:, :], ACT.Copy).then_inc(y_copied, 1)

            def body(c, j, n, recur, had, gate, down):
                for s_ in range(SLOTS):
                    if recur:
                        stage(n, s_)
                    ffn(c, j, n, s_, had, gate, down)

            run_bodies(act, body)

        @block.tensor
        def _(pe):
            pe.wait_ge(ident_in, 16)
            pe.wait_ge(ones_set, 1)
            for i in range(2):
                pe.wait_ge(peaks_found, i + 1)
                pe.transpose(ps_had[0:1, 0:P], peak[:, i:i + 1], ident[:, :]).then_inc(peaks_turned, 1)
                pe.wait_ge(top_found, i + 1)
                pe.matmul(ps_had[:, 0:1], ones[:, :], top[:, 2 * i + 1:2 * i + 2],
                          start=True, stop=True).then_inc(top_spread, 1)
            pe.wait_ge(had_in, 16)
            pe.wait_ge(fly_add, 4)
            pe.wait_ge(fly_sub, 4)
            for i in range(IT):
                if i >= 2:
                    pe.wait_ge(wd_copied, i - 1)
                pe.matmul([ps_gate, ps_up][i % 2][:, :], h128[:, :], raw[:, i * N:(i + 1) * N],
                          start=True, stop=True).then_inc(wd_rotated, 1)
            pe.wait_ge(wsd_in, 16)
            pe.wait_ge(unscale_set, 2)
            pe.matmul(ps_had[:, :], ones[:, :], wsd_row[:, :], start=True, stop=True).then_inc(wsd_spread, 1)
            pe.wait_ge(wsd_set, 1)
            pe.wait_ge(had_set, 1)
            pe.wait_ge(c_lo_split, 1)
            pe.wait_ge(wd_lo_split, IT)

            def stage(n, s):
                g = n * SLOTS + s
                pe.wait_ge(kq_ready, g + 1)
                pe.wait_ge(thi_ready, g + 1)
                for m in range(KT):
                    for kt in range(KT):
                        pe.matmul(prod[:, 0, m * B:(m + 1) * B], c_lo[:, kt, m * P:(m + 1) * P],
                                  t_parts[:, kt, 0, :], start=(m == 0 and kt == 0), stop=False,
                                  skip_group_check=True)
                pe.wait_ge(tlo_ready, g + 1)
                for m in range(KT):
                    for kt in range(KT):
                        last = pe.matmul(prod[:, :, m * B:(m + 1) * B],
                                         c_hi[:, kt, m * P:(m + 1) * P], t_parts[:, kt, :, :],
                                         start=False, stop=(m == KT - 1 and kt == KT - 1),
                                         skip_group_check=True)
                last.then_inc(prod_ready, 1)

            def parts(hi, lo):
                return ((0, 0), (0, 1), (1, 0))

            def ffn(c, j, n, s, had, gate, down):
                if gate:
                    h = (n - 17) // BODIES
                    tile = (n - 17) % BODIES
                    parity = h % 2
                    w = (wg_hi, wg_lo) if s < 4 else (wu_hi, wu_lo)
                    bank, ready = (ps_gate, gate_done) if s < 4 else (ps_up, up_done)
                    kt = s % 4
                    if s == 0:
                        pe.wait_ge(sil_ready, n - 17)
                    if s == 4:
                        pe.wait_ge(up_ready, n - 17)
                    if isinstance(j, int) and j == 1 and s in (0, 2):
                        pe.wait_ge(xhi_ready, KT * (c - 1) + s + 2)
                        pe.wait_ge(xlo_ready, KT * (c - 1) + s + 2)
                    for x, (a, b) in enumerate(((0, 0), (1, 0), (0, 1))):
                        xs = (xh_hi_f, xh_lo_f)[b]
                        last = pe.matmul(bank[:, 0:ROWS],
                                         w[a][:, bass.ds(tile * P + kt * INTER, P)],
                                         xs[:, bass.ds(parity * (KT * ROWS) + kt * ROWS, ROWS)],
                                         start=(kt == 0 and x == 0), stop=(kt == 3 and x == 2))
                    if kt == 3:
                        last.then_inc(ready, 1)
                if down and s >= 2:
                    a = (s - 2) // 3
                    x = (s - 2) % 3
                    tile = (n - 18) % IT
                    if s == 2:
                        pe.wait_ge(hidhi_ready, n - 17)
                        pe.wait_ge(hidlo_ready, n - 17)
                    first = isinstance(j, int) and j == 2
                    end = isinstance(j, int) and j == 1
                    if first and x == 0 and not (isinstance(c, int) and c == 1):
                        pe.wait_ge(y_copied, RT * (c - 2) + a + 1)
                    last = pe.matmul(ps_y[a][:, :], (hid_hi, hid_hi, hid_lo)[x][:, a * P:(a + 1) * P],
                                     (wd_hi, wd_lo, wd_hi)[x][:, bass.ds(tile * N, N)],
                                     start=(first and x == 0), stop=(end and x == 2),
                                     skip_group_check=True)
                    if s == 7:
                        last.then_inc(down_done, 1)
                if had and s in (1, 2, 4, 5):
                    half = s // 4
                    if s == 1:
                        pe.wait_ge(qlo_ready, c * CHUNK_STEPS + 1)
                        pe.wait_ge(wsd_set, 1)
                    if s == 4:
                        pe.wait_ge(xf_ready, KT * (c - 1) + 2)
                    if s == 1 and not (isinstance(c, int) and c == 1):
                        pe.wait_ge(xf_ready, KT * (c - 1))
                    o = (s - 1) % 3
                    m = 2 * half + o
                    for kt in range(KT):
                        sign = bin(m & kt).count("1") % 2
                        for part in range(2):
                            base = q_parts[:, bass.ds(((c - 1) * CHUNK_STEPS + 1) * 2 * SW,
                                                      CHUNK_STEPS * 2 * SW)]
                            rows = base.rearrange("p (t a k b) -> p t a k b", a=2, k=KT,
                                                  b=B)[:, :, part, kt, :]
                            last = pe.matmul(ps_had[:, o * ROWS:(o + 1) * ROWS].rearrange(
                                                 "p (t b) -> p t b", b=B),
                                             (had_m if sign else had_p)[:, kt, :], rows,
                                             start=(kt == 0 and part == 0 and o == 0), stop=(kt == 3 and part == 1 and o == 1),
                                             skip_group_check=True)
                    if o == 1:
                        last.then_inc(had_done, 1)

            def body(c, j, n, recur, had, gate, down):
                for s_ in range(SLOTS):
                    if recur:
                        stage(n, s_)
                    ffn(c, j, n, s_, had, gate, down)

            run_bodies(pe, body)

        @block.vector
        def _(dve):
            dve.memset(ones[:, :], 1.0).then_inc(ones_set, 1)
            dve.memset(warm[:, :], 0.0).then_inc(ones_set, 1)
            dve.wait_ge(raw_in, 16)
            c_hi_f, c_lo_f = [c[:, :, :].rearrange("p k n -> p (k n)") for c in (c_hi, c_lo)]
            dve.tensor_scalar(c_hi_f, c_raw, S, None, ALU.mult).then_inc(c_hi_split, 1)
            dve.wait_ge(c_hi_split, 1)
            dve.scalar_tensor_tensor(out=c_lo_f, in0=c_raw, scalar=S, in1=c_hi_f, op0=ALU.mult,
                                     op1=ALU.subtract).then_inc(c_lo_split, 1)
            dve.wait_ge(c_lo_split, 1)
            dve.memset(rec[:, 0:1], 0.0).then_inc(raw_free, 1)
            dve.wait_ge(vec_in, 16)
            dve.wait_ge(drive_in, 16)
            dve.tensor_scalar(bias[:, :], vec[:, V_BIAS:V_BIAS + KT], P_SHIFT, None,
                              ALU.subtract).then_inc(bias_set, 1)
            dve.wait_ge(bias_set, 1)
            drive_v = drive[:, 0:T * SW].rearrange("p (t k b) -> p t k b", k=KT, b=B)
            for kt in range(KT):
                dve.tensor_scalar(drive_v[:, :, kt, :], drive_v[:, :, kt, :],
                                  bias[:, kt:kt + 1], S, ALU.add,
                                  ALU.mult).then_inc(drive_set, 1)
            dve.wait_ge(had_in, 16)
            for kt in range(KT):
                sign = vec[:, V_SUUG + kt:V_SUUG + kt + 1]
                dve.tensor_scalar(had_p[:, kt, :], h128[:, :], sign, None, ALU.mult)
                last = dve.tensor_scalar(had_m[:, kt, :], h128[:, :], sign, -1.0, ALU.mult, ALU.mult)
            last.then_inc(had_set, 1)
            for i, (hi, lo) in enumerate(((wu_hi, wu_lo), (wg_hi, wg_lo))):
                dve.wait_ge(raw_in, 32 + 16 * i)
                dve.tensor_reduce(peak[:, i:i + 1], raw[:, :], AX.X, ALU.max,
                                  apply_absolute_value=True).then_inc(peaks_found, 1)
                dve.wait_ge(peaks_turned, i + 1)
                dve.tensor_reduce(top[:, 2 * i:2 * i + 1], ps_had[0:1, 0:P], AX.X,
                                  ALU.max).then_inc(scales_step, 1)
                dve.wait_ge(scales_step, 2 * i + 1)
                dve.tensor_scalar(top[:, 2 * i + 1:2 * i + 2], top[:, 2 * i:2 * i + 1],
                                  1.0 / FP16_TOP, 1e-30, ALU.mult, ALU.max).then_inc(top_found, 1)
                dve.wait_ge(top_spread, i + 1)
                dve.tensor_copy(unscale[:, i:i + 1], ps_had[:, 0:1]).then_inc(unscale_set, 1)
                dve.wait_ge(unscale_set, i + 1)
                dve.reciprocal(wscale[:, i:i + 1], unscale[:, i:i + 1]).then_inc(scale_set, 1)
                dve.wait_ge(w_hi_split, i + 1)
                dve.scalar_tensor_tensor(out=lo[:, :], in0=raw[:, :], scalar=wscale[:, i:i + 1],
                                         in1=hi[:, :], op0=ALU.mult,
                                         op1=ALU.subtract).then_inc(w_lo_split, 1)
                dve.wait_ge(w_lo_split, i + 1)
                dve.memset(top[:, 2 * i:2 * i + 1], 0.0).then_inc(raw_free, 1)
                dve.wait_ge(raw_free, i + 2)
                dve.memset(utmp[:, :, :], 0.0).then_inc(scales_step, 1)
            dve.wait_ge(raw_in, 64)
            for lv in range(4):
                src, dst = (raw, wd_buf) if lv % 2 == 0 else (wd_buf, raw)
                w = (1 << lv) * N
                sv = src[:, :].rearrange("p (g a w) -> p g a w", a=2, w=w)
                dv = dst[:, :].rearrange("p (g a w) -> p g a w", a=2, w=w)
                if lv:
                    dve.wait_ge(fly_add, lv)
                    dve.wait_ge(fly_sub, lv)
                dve.tensor_tensor(dv[:, :, 0, :], sv[:, :, 0, :], sv[:, :, 1, :],
                                  ALU.add).then_inc(fly_add, 1)
            dve.wait_ge(wd_copied, IT)
            dve.tensor_reduce(dpeak[:, :], raw[:, :].rearrange("p (i n) -> p i n", n=N), AX.X,
                              ALU.max, apply_absolute_value=True).then_inc(scales_step, 1)
            dve.wait_ge(scales_step, 5)
            dve.tensor_scalar(dunscale[:, :], dpeak[:, :], 1.0 / FP16_TOP, 1e-30, ALU.mult,
                              ALU.max).then_inc(d_unscale_set, 1)
            dve.wait_ge(d_unscale_set, 1)
            dve.reciprocal(dscale[:, :], dunscale[:, :]).then_inc(d_scale_set, 1)
            root = float(N) ** -0.5
            dve.tensor_scalar(gscale[:, :], vec[:, V_WGATE:V_WGATE + IT], unscale[:, 1:2], root,
                              ALU.mult, ALU.mult)
            dve.tensor_scalar(utmp[:, 0, :], vec[:, V_WUP:V_WUP + IT], unscale[:, 0:1],
                              root * float(INTER) ** -0.5, ALU.mult, ALU.mult).then_inc(scales_step, 1)
            dve.wait_ge(scales_step, 6)
            dve.tensor_tensor(utmp[:, 1, :], utmp[:, 0, :], vec[:, V_SUDP:V_SUDP + IT],
                              ALU.mult).then_inc(scales_step, 1)
            dve.wait_ge(scales_step, 7)
            dve.tensor_tensor(uscale[:, :], utmp[:, 1, :], dunscale[:, :],
                              ALU.mult).then_inc(scales_step, 1)
            for i in range(IT):
                dve.wait_ge(wd_hi_split, i + 1)
                dve.scalar_tensor_tensor(out=wd_lo[:, i * N:(i + 1) * N],
                                         in0=raw[:, i * N:(i + 1) * N], scalar=dscale[:, i:i + 1],
                                         in1=wd_hi[:, i * N:(i + 1) * N], op0=ALU.mult,
                                         op1=ALU.subtract).then_inc(wd_lo_split, 1)
            dve.wait_ge(cond_in, 16)
            dve.wait_ge(scales_step, 8)
            dve.memset(kq[:, 3, :], 0.0).then_inc(kq_ready, 1)
            dve.memset(ksum[:, :], 0.0).then_inc(q_ready, 1)
            dve.tensor_scalar(r[:, 0, :], q[:, :], S / AQ[0], None, ALU.mult).then_inc(r_ready, 1)

            def stage(n, s):
                i = s % 4
                g = n * SLOTS + s
                st = n * BODY_STEPS + s // 4
                drive_now = drive[:, bass.ds(st * SW, SW)]
                c = A[i] * EPSILON

                if i == 0:
                    dve.wait_ge(r_ready, g + 1)
                    dve.tensor_scalar(r_clip[:, :], r[:, 0, :], CLAMP * S / AQ[0],
                                      -CLAMP * S / AQ[0], ALU.min, ALU.max).then_inc(rclip_ready, 1)
                    src = r_clip[:, :]
                    dve.wait_ge(rclip_ready, st + 1)
                else:
                    src = r[:, i, :]
                    dve.wait_ge(r_ready, g + 1)
                dve.scalar_tensor_tensor(out=q_sq[:, i, :], in0=src, scalar=-(AQ[i] / S) ** 2 / 3,
                                         in1=src, op0=ALU.mult, op1=ALU.mult).then_inc(sq_ready, 1)
                if i == 0:
                    dve.wait_ge(push0_ready, st + 1)
                    dve.scalar_tensor_tensor(out=push_old[:, 0, :], in0=p[:, :], scalar=c * BETA,
                                             in1=push[:, 0, :], op0=ALU.mult,
                                             op1=ALU.add).then_inc(old_ready, 1)
                elif i < 3:
                    dve.wait_ge(push_ready, 3 * st + i)
                    dve.wait_ge(base_ready, 2 * st + i)
                    dve.scalar_tensor_tensor(out=push_old[:, i, :], in0=push[:, i, :],
                                             scalar=-c * BETA, in1=push_base[:, i - 1, :],
                                             op0=ALU.mult, op1=ALU.add).then_inc(old_ready, 1)
                else:
                    dve.wait_ge(ksump_ready, st + 1)
                    dve.wait_ge(kq_ready, g + 1)
                    dve.scalar_tensor_tensor(out=push_last[:, :], in0=kq[:, 2, :], scalar=2.0,
                                             in1=ksum_push[:, :], op0=ALU.mult,
                                             op1=ALU.add).then_inc(last_ready, 1)
                dve.wait_ge(sq_ready, g + 1)
                dve.scalar_tensor_tensor(out=fq[:, i, :], in0=q_sq[:, i, :], scalar=1.0, in1=src,
                                         op0=ALU.add, op1=ALU.mult).then_inc(fq_ready, 1)
                if i < 3:
                    now, unit = (q[:, :], S) if i == 0 else (r[:, i, :], AQ[i])
                    if i == 0:
                        dve.wait_ge(q_ready, st + 1)
                    dve.wait_ge(old_ready, 3 * st + i + 1)
                    dve.scalar_tensor_tensor(out=push[:, i + 1, :], in0=now, scalar=-c * unit,
                                             in1=push_old[:, i, :], op0=ALU.mult,
                                             op1=ALU.add).then_inc(push_ready, 1)
                if i == 2:
                    dve.wait_ge(kq_ready, g + 1)
                    dve.scalar_tensor_tensor(out=ksum[:, :], in0=kq[:, 1, :], scalar=2.0,
                                             in1=kq[:, 0, :], op0=ALU.mult,
                                             op1=ALU.add).then_inc(ksum_ready, 1)
                if i == 3:
                    dve.wait_ge(last_ready, st + 1)
                dve.wait_ge(fq_ready, g + 1)
                dve.scalar_tensor_tensor(out=b_small, in0=fq[:, i, :], scalar=AQ[i],
                                         in1=(push_last[:, :] if i == 3 else push[:, i, :]),
                                         op0=ALU.mult, op1=ALU.add).then_inc(bsmall_ready, 1)
                if i < 2:
                    dve.scalar_tensor_tensor(out=push_base[:, i, :], in0=drive_now,
                                             scalar=A[i + 1] * EPSILON * BETA, in1=push[:, 0, :],
                                             op0=ALU.mult, op1=ALU.add).then_inc(base_ready, 1)
                dve.wait_ge(tfull_ready, g + 1)
                dve.tensor_tensor(t_parts[:, :, 1, :], t_full[:, :].rearrange("p (k b) -> p k b", k=KT),
                                  t_parts[:, :, 0, :], ALU.subtract).then_inc(tlo_ready, 1)
                dve.wait_ge(bsmall_ready, g + 1)
                dve.scalar_tensor_tensor(out=b_full, in0=q[:, :], scalar=S / A[i], in1=b_small,
                                         op0=ALU.mult, op1=ALU.add).then_inc(bfull_ready, 1)
                dve.wait_ge(prod_ready, g + 1)
                dve.wait_ge(bfull_ready, g + 1)
                dve.tensor_reduce(r[:, (i + 1) % 4, :], sum_full, AX.X, ALU.add).then_inc(r_ready, 1)
                dve.tensor_reduce(kq[:, i, :], sum_small, AX.X, ALU.add).then_inc(kq_ready, 1)

            def step_end(n, s):
                st = n * BODY_STEPS + s // 4
                dve.wait_ge(kq_ready, n * SLOTS + s + 2)
                dve.scalar_tensor_tensor(out=q_raw[:, :], in0=kq[:, 3, :], scalar=A[3] / S,
                                         in1=q[:, :], op0=ALU.mult,
                                         op1=ALU.add).then_inc(qraw_ready, 1)
                dve.wait_ge(qraw_ready, st + 1)
                dve.wait_ge(ppart_ready, 5 * st + 2)
                dve.wait_ge(qlo_ready, st + 1)
                dve.tensor_scalar(q[:, :], q_raw[:, :], CLAMP, -CLAMP, ALU.min,
                                  ALU.max).then_inc(q_ready, 1)

            def body(c, j, n, recur, had, gate, down):
                for s_ in range(SLOTS):
                    if recur:
                        stage(n, s_)
                        if s_ % 4 == 3:
                            step_end(n, s_)

            with dve.Fori(0, CHUNKS * BODIES) as n:
                body(None, None, n, True, False, False, False)

        @block.gpsimd
        def _(pool):
            pool.wait_ge(cond_in, 16)
            pool.tensor_scalar(p[:, :], q[:, :], S, -S * P_SHIFT, ALU.mult,
                               ALU.add).then_inc(p_ready, 1)
            for i in range(4):
                pool.memset(p_weight[:, i, :], P_FROM[i] * (AQ[i] if i else S)).then_inc(weight_set, 1)
            pool.wait_ge(weight_set, 4)
            pool.wait_ge(raw_in, 64)
            for lv in range(4):
                src, dst = (raw, wd_buf) if lv % 2 == 0 else (wd_buf, raw)
                w = (1 << lv) * N
                sv = src[:, :].rearrange("p (g a w) -> p g a w", a=2, w=w)
                dv = dst[:, :].rearrange("p (g a w) -> p g a w", a=2, w=w)
                if lv:
                    pool.wait_ge(fly_add, lv)
                    pool.wait_ge(fly_sub, lv)
                pool.tensor_tensor(dv[:, :, 1, :], sv[:, :, 0, :], sv[:, :, 1, :],
                                   ALU.subtract).then_inc(fly_sub, 1)
            pool.wait_ge(drive_set, KT)

            def wait_apart(signal, count):
                count = pool.snap(count) if not isinstance(count, int) else count
                pool.wait_ge(cond_in, 16)
                pool.wait_ge(signal, count)

            def q_split(st):
                slot = q_parts[:, bass.ds(st * 2 * SW, 2 * SW)]
                pool.tensor_copy(slot[:, 0:SW], q[:, :]).then_inc(qhi_ready, 1)
                wait_apart(qhi_ready, st + 1)
                pool.tensor_tensor(slot[:, SW:2 * SW], q[:, :], slot[:, 0:SW],
                                   ALU.subtract).then_inc(qlo_ready, 1)

            def stage(n, s):
                i = s % 4
                g = n * SLOTS + s
                st = n * BODY_STEPS + s // 4
                if i == 0:
                    wait_apart(p_ready, st + 1)
                    pool.tensor_tensor(push[:, 0, :], drive[:, bass.ds(st * SW, SW)], p[:, :],
                                       ALU.subtract).then_inc(push0_ready, 1)
                    pool.tensor_scalar(p_part[:, 4, :], p[:, :], P_SELF, None,
                                       ALU.mult).then_inc(ppart_ready, 1)
                    pool.wait_ge(q_ready, st + 1)
                    now = q[:, :]
                else:
                    pool.wait_ge(r_ready, g + 1)
                    now = r[:, i, :]
                pool.tensor_tensor(p_part[:, i, :], now, p_weight[:, i, :],
                                   ALU.mult).then_inc(ppart_ready, 1)
                pool.wait_ge(ppart_ready, 5 * st + i + 2)
                if i:
                    pool.wait_ge(pacc_ready, 4 * st + i)
                pool.tensor_tensor(p_acc[:, i, :], p_part[:, 4, :] if i == 0 else p_acc[:, i - 1, :],
                                   p_part[:, i, :], ALU.add).then_inc(pacc_ready, 1)
                if i == 1:
                    wait_apart(base_ready, 2 * st + 2)
                    q_split(st)
                if i == 2:
                    pool.wait_ge(push_ready, 3 * st + 3)
                    pool.wait_ge(ksum_ready, st + 1)
                    pool.tensor_tensor(ksum_push[:, :], ksum[:, :], push[:, 3, :],
                                       ALU.add).then_inc(ksump_ready, 1)
                if i == 3:
                    pool.wait_ge(pacc_ready, 4 * st + 4)
                    pool.tensor_tensor(p_raw[:, :], p[:, :], p_acc[:, 3, :],
                                       ALU.add).then_inc(praw_ready, 1)
                    wait_apart(praw_ready, st + 1)
                    pool.tensor_scalar(p[:, :], p_raw[:, :], (CLAMP - P_SHIFT) * S,
                                       (-CLAMP - P_SHIFT) * S, ALU.min, ALU.max).then_inc(p_ready, 1)

            def ffn(c, j, n, s, had, gate, down):
                if down and s == 0:
                    pool.wait_ge(up_ready, n - 17)
                    pool.wait_ge(sil_ready, n - 17)
                    pool.wait_ge(hidhi_ready, n - 18)
                    pool.wait_ge(hidlo_ready, n - 18)
                    pool.tensor_tensor(hid[:, :], up[:, :], sil[:, :], ALU.mult).then_inc(hid_ready, 1)
                if down and s == 1:
                    pool.wait_ge(hidhi_ready, n - 17)
                    pool.wait_ge(hid_ready, n - 17)
                    pool.wait_ge(down_done, n - 18)
                    pool.tensor_tensor(hid_lo[:, :], hid[:, :], hid_hi[:, :],
                                       ALU.subtract).then_inc(hidlo_ready, 1)
                if had and s in (3, 6):
                    half = s // 4
                    h = c - 1
                    for i in range(2):
                        x = KT * h + 2 * half + i + 1
                        at = (h % 2) * (KT * ROWS) + (2 * half + i) * ROWS
                        wait_apart(xf_ready, x)
                        pool.tensor_copy(xh_hi_f[:, bass.ds(at, ROWS)], xf[:, i, :]).then_inc(xhi_ready, 1)
                        wait_apart(xhi_ready, x)
                        pool.tensor_tensor(xh_lo_f[:, bass.ds(at, ROWS)], xf[:, i, :],
                                           xh_hi_f[:, bass.ds(at, ROWS)],
                                           ALU.subtract).then_inc(xlo_ready, 1)
                if isinstance(j, int) and j == 2 and s in (3, 5) and not (isinstance(c, int) and c == 1):
                    a = (s - 3) // 2
                    v = RT * (c - 2) + a + 1
                    pool.wait_ge(y_copied, v)
                    pool.tensor_tensor(y_sb[:, a, :], y_sb[:, a, :], wsd_all[:, :],
                                       ALU.mult).then_inc(y_scaled, 1)
                    pool.wait_ge(y_scaled, v)
                    pool.wait_ge(x_in, 16 * (c - 1))
                    pool.tensor_tensor(y_sb[:, a, :], y_sb[:, a, :], x_res[:, a, :],
                                       ALU.add).then_inc(y_ready, 1)

            def body(c, j, n, recur, had, gate, down):
                for s_ in range(SLOTS):
                    if recur:
                        stage(n, s_)
                    ffn(c, j, n, s_, had, gate, down)

            def last_split():
                pool.wait_ge(q_ready, T + 1)
                q_split(T)

            run_bodies(pool, body, last_split)


def _hadamard():
    h = np.ones((1, 1), np.float32)
    while h.shape[0] < P:
        h = np.block([[h, h], [h, -h]])
    return np.ascontiguousarray(h.astype(np.float32))


def kernel(x, cond_2048, L0_cond_coupling, L0_cond_bias, L0_ffn_SU_ug, L0_ffn_SU_dp,
           L0_ffn_Wscale_ug, L0_ffn_Wscale_dp, L0_ffn_W_up, L0_ffn_W_gate, L0_ffn_W_down):
    import concourse.bacc as bacc
    from concourse.bass_utils import run_bass_kernel_spmd

    def columns(v):
        return np.asarray(v).reshape(-1, P).T

    x = np.asarray(x)
    arrays = {
        "x_state": x.reshape(B, T, KT, P).transpose(3, 1, 2, 0).reshape(P, T * SW),
        "x_rows": x.transpose(1, 0, 2).reshape(T * B, N),
        "cond": np.asarray(cond_2048).reshape(B, KT, P).transpose(2, 1, 0).reshape(P, SW),
        "coupling": np.asarray(L0_cond_coupling).T,
        "w_up": np.asarray(L0_ffn_W_up).T,
        "w_gate": np.asarray(L0_ffn_W_gate).T,
        "w_down": np.asarray(L0_ffn_W_down).T,
        "vectors": np.concatenate([columns(L0_cond_bias), columns(L0_ffn_SU_ug),
                                   columns(L0_ffn_Wscale_ug), columns(L0_ffn_SU_dp)], axis=1),
        "ws_down": np.asarray(L0_ffn_Wscale_dp).reshape(1, N),
        "hadamard": _hadamard(),
        "identity": np.eye(P, dtype=np.float32),
    }
    arrays = {n: np.ascontiguousarray(a) for n, a in arrays.items()}
    nc = bacc.Bacc("TRN2", target_bir_lowering=False, num_devices=1)
    args = {n: nc.dram_tensor("in_" + n, a.shape, mybir.dt.from_np(a.dtype), kind="ExternalInput").ap()
            for n, a in arrays.items()}
    out = nc.dram_tensor("out_rows", (T * B, N), F32, kind="ExternalOutput").ap()
    build(nc, out=out, **args)
    res = run_bass_kernel_spmd(nc, [{"in_" + n: a for n, a in arrays.items()}], core_ids=[0])
    rows = res.results[0]["out_rows"]
    return np.ascontiguousarray(rows.reshape(T, B, N).transpose(1, 0, 2))
```

```python
from contextlib import ExitStack

import numpy as np

import concourse.bass as bass
from concourse import mybir

F32 = mybir.dt.float32
F16 = mybir.dt.float16
BF16 = mybir.dt.bfloat16
ALU = mybir.AluOpType
ACT = mybir.ActivationFunctionType
AX = mybir.AxisListType

P = 128
B = 8
T = 256
N = 512
INTER = 2048
KT = N // P
IT = INTER // P
SW = KT * B
HW = SW // 2

DT = 0.01
EPSILON = 0.08
ALPHA = 0.7
BETA = 0.8
CLAMP = 20.0
S = 64.0
A = [DT / 2, DT / 2, DT, DT / 6]
P_SHIFT = ALPHA / BETA
_E, _Z = EPSILON * DT, EPSILON * BETA * DT
P_SELF = -_Z + _Z ** 2 / 2 - _Z ** 3 / 6 + _Z ** 4 / 24
P_FROM = [_E / 6 * (1 - _Z + _Z ** 2 / 2 - _Z ** 3 / 4), _E / 6 * (2 - _Z + _Z ** 2 / 2),
          _E / 6 * (2 - _Z), _E / 6]
AQ = [A[3], A[0], A[1], A[2]]
BASE = [float(np.float32(AQ[0] / a)) for a in A[:3]]
BASE_EXCESS = BASE[0] + 2 * BASE[1] + 2 * BASE[2] - 1
assert float(np.float32(BASE_EXCESS)) == BASE_EXCESS

BODY_STEPS = 2
SLOTS = 4 * BODY_STEPS
ROWS = 256
RT = ROWS // P
CHUNK_STEPS = ROWS // B
CHUNKS = T // CHUNK_STEPS
BODIES = CHUNK_STEPS // BODY_STEPS
assert BODIES == IT
GU_SHARE = [5, 5, 5, 4, 5, 0, 0, 0]
DOWN_SLOTS = [5, 5, 6, 6, 7, 7]
FILL_SLOTS = [3, 5, 6, 7]
assert sum(GU_SHARE) == 2 * 3 * KT
FP16_TOP = 1024.0

V_BIAS, V_SUUG, V_WUP, V_WGATE, V_SUDP, V_COLS = 0, 4, 8, 24, 40, 56


def build(nc, x_state, x_rows, cond, coupling, w_up, w_gate, w_down, vectors, ws_down, hadamard,
          identity, out):
    with ExitStack() as ctx:
        def sb(name, shape, dt=F32):
            return ctx.enter_context(nc.sbuf_tensor(name, shape, dt))

        def sem(name):
            return ctx.enter_context(nc.semaphore(name))

        raw = sb("raw", [P, IT * N])
        c_raw = raw[:, 0:KT * N]
        c_hi = sb("c_hi", [P, KT, N], F16)
        c_lo = sb("c_lo", [P, KT, N], F16)
        wu_hi = sb("wu_hi", [P, KT * INTER], F16)
        wu_lo = sb("wu_lo", [P, KT * INTER], F16)
        wg_hi = sb("wg_hi", [P, KT * INTER], F16)
        wg_lo = sb("wg_lo", [P, KT * INTER], F16)
        wd_buf = sb("wd_buf", [P, IT * N])
        wd_parts = wd_buf[:, :].bitcast(F16)
        wd_hi = wd_parts[:, 0:IT * N]
        wd_lo = wd_parts[:, IT * N:2 * IT * N]
        vec = sb("vec", [P, V_COLS])
        h128 = sb("h128", [P, P])
        ident = sb("ident", [P, P])
        ones = sb("ones", [1, P])
        wsd_row = sb("wsd_row", [1, N])
        wsd_all = sb("wsd_all", [P, N])
        had_p = sb("had_p", [P, KT, P], F16)
        had_m = sb("had_m", [P, KT, P], F16)
        peak = sb("peak", [P, 2])
        top = sb("top", [1, 4])
        unscale = sb("unscale", [P, 2])
        wscale = sb("wscale", [P, 2])
        dpeak = sb("dpeak", [P, IT])
        dunscale = sb("dunscale", [P, IT])
        dscale = sb("dscale", [P, IT])
        gscale = sb("gscale", [P, IT])
        uscale = sb("uscale", [P, IT])
        utmp = sb("utmp", [P, 2, IT])
        warm = sb("warm", [P, 1])
        bias = sb("bias", [P, KT])

        track = sb("track", [P, (T + 2) * SW])
        drive = track[:, SW:]
        q_parts = track[:, :].bitcast(F16)
        t_parts = sb("t_parts", [P, KT, 2, B], F16)
        t_full = sb("t_full", [P, SW])
        r = sb("r", [P, 4, SW])
        r_clip = sb("r_clip", [P, SW])
        q_cond = sb("q_cond", [P, SW])
        q_sq = sb("q_sq", [P, 4, SW])
        fq = sb("fq", [P, 4, SW])
        base_push = sb("base_push", [P, 4, SW])
        r_acc = sb("r_acc", [P, 2, SW])
        acc_push = sb("acc_push", [P, SW])
        p = sb("p", [P, 3, SW])
        p_raw = sb("p_raw", [P, SW])
        p_decay = sb("p_decay", [P, 3, SW])
        p_drive = sb("p_drive", [P, 3, SW])
        p_move = sb("p_move", [P, 3, SW])
        p_part = sb("p_part", [P, 5, SW])
        p_acc = sb("p_acc", [P, 4, SW])
        push = sb("push", [P, 4, SW])

        xh_hi = sb("xh_hi", [P, 2, KT * ROWS], F16)
        xh_lo = sb("xh_lo", [P, 2, KT * ROWS], F16)
        xh_hi_f = xh_hi[:, :, :].rearrange("p a b -> p (a b)")
        xh_lo_f = xh_lo[:, :, :].rearrange("p a b -> p (a b)")
        sil = sb("sil", [P, ROWS])
        hid = sb("hid", [P, ROWS])
        hid_hi = sb("hid_hi", [P, ROWS], BF16)
        hid_lo = sb("hid_lo", [P, ROWS], BF16)
        x_res = sb("x_res", [P, RT, N])
        y_sb = sb("y_sb", [P, RT, N])

        rec = ctx.enter_context(nc.psum_tensor("rec", [P, 3 * 512], F32))
        prod = [rec[:, o:o + 512].rearrange("p (s c) -> p s c", s=2) for o in (0, 1024)]
        sum_full = [rec[:, o:o + 768].rearrange("p (s c) -> p c s", s=3)[:, 0:HW, :]
                    for o in (0, 768)]
        b_full = rec[:, 512:1024].rearrange("p (h c) -> p h c", h=2)[:, :, 0:HW]

        def halves(ap):
            return ap.rearrange("p (h c) -> p h c", h=2)

        def half(ap, x):
            return ap[:, x * HW:(x + 1) * HW]

        ps_gate, ps_up, ps_had, ps_y0, ps_y1 = [
            ctx.enter_context(nc.psum_tensor(n, [P, 512], F32))
            for n in ("ps_gate", "ps_up", "ps_had", "ps_y0", "ps_y1")]
        ps_y = [ps_y0, ps_y1]

        vec_in, had_in, ident_in, cond_in, drive_in, wsd_in = [
            sem(n) for n in ("vec_in", "had_in", "ident_in", "cond_in", "drive_in", "wsd_in")]
        raw_in, raw_free, peaks_found, peaks_turned, top_found, top_spread, scale_set, \
            unscale_set, w_hi_split, w_lo_split = [
                sem(n) for n in ("raw_in", "raw_free", "peaks_found", "peaks_turned", "top_found",
                                 "top_spread", "scale_set", "unscale_set", "w_hi_split",
                                 "w_lo_split")]
        fly_add, fly_sub, wd_rotated, wd_scaled, d_unscale_set, d_scale_set, wd_hi_split, \
            wd_lo_split = [
                sem(n) for n in ("fly_add", "fly_sub", "wd_rotated", "wd_scaled", "d_unscale_set",
                                 "d_scale_set", "wd_hi_split", "wd_lo_split")]
        c_hi_split, c_lo_split, ones_set, wsd_spread, wsd_set, had_set, drive_set, scales_step, \
            table_warm, bias_set = [
                sem(n) for n in ("c_hi_split", "c_lo_split", "ones_set", "wsd_spread", "wsd_set",
                                 "had_set", "drive_set", "scales_step", "table_warm",
                                 "bias_set")]
        def sem_set(name, *shape):
            if not shape:
                return sem(name)
            return [sem_set(f"{name}_{i}", *shape[1:]) for i in range(shape[0])]

        r_ready, thi_ready, tfull_ready, tlo_ready, prod_ready = [
            sem_set(n, 4, 2) for n in ("r_ready", "thi_ready", "tfull_ready", "tlo_ready",
                                       "prod_ready")]
        sq_ready, fq_ready, bpush_ready, bfull_ready, ppart_ready, pacc_ready, push_ready = [
            sem_set(n, 4) for n in ("sq_ready", "fq_ready", "bpush_ready", "bfull_ready",
                                    "ppart_ready", "pacc_ready", "push_ready")]
        pdecay_ready, pdrive_ready, pmove_ready, pnext_ready = [
            sem_set(n, 3) for n in ("pdecay_ready", "pdrive_ready", "pmove_ready", "pnext_ready")]
        rclip_ready, acc1_ready, acc2_ready, accpush_ready, pself_ready, praw_ready, p_ready, \
            qhi_ready, qlo_ready = [
                sem(n) for n in ("rclip_ready", "acc1_ready", "acc2_ready", "accpush_ready",
                                 "pself_ready", "praw_ready", "p_ready", "qhi_ready",
                                 "qlo_ready")]
        had_done, xhi_ready, xlo_ready, y_ready, x_in, out_done = [
            sem(n) for n in ("had_done", "xhi_ready", "xlo_ready", "y_ready", "x_in", "out_done")]
        gate_done, up_done, sil_ready, hid_ready, hidhi_ready, hidlo_ready, down_done = [
            sem(n) for n in ("gate_done", "up_done", "sil_ready", "hid_ready",
                             "hidhi_ready", "hidlo_ready", "down_done")]

        block = ctx.enter_context(nc.Block())

        def step_counts(eng, n):
            counts = [n * BODY_STEPS + k + 1 for k in range(BODY_STEPS)]
            return counts if isinstance(n, int) else [eng.snap(c) for c in counts]

        def run_bodies(eng, body, idle=None, group=1):
            lead = 3 if group == 1 else 4

            def chunk(c, recur):
                one = isinstance(c, int) and c == 1
                body(c, 0, c * BODIES, recur, True, not one, not one, follows=False)
                body(c, 1, c * BODIES + 1, recur, False, True, not one, follows=True)
                for j in range(2, lead):
                    body(c, j, c * BODIES + j, recur, False, True, True, follows=True)
                with eng.Fori(0, (BODIES - lead) // group) as turn:
                    for k in range(group):
                        j = turn * group + (lead + k)
                        body(c, j, c * BODIES + j, recur, False, True, True, follows=k > 0)

            first = 0
            if group > 1:
                first = 1
                body(0, None, 0, True, False, False, False, follows=False)
            assert (BODIES - first) % group == 0 and (BODIES - lead) % group == 0
            with eng.Fori(0, (BODIES - first) // group) as turn:
                for k in range(group):
                    body(0, None, turn * group + (first + k), True, False, False, False, follows=k > 0)
            chunk(1, True)
            with eng.Fori(2, CHUNKS) as c:
                chunk(c, True)
            if idle:
                idle()
            chunk(CHUNKS, False)
            c = CHUNKS + 1
            body(c, 0, c * BODIES, False, False, True, True, follows=False)
            body(c, 1, c * BODIES + 1, False, False, False, True, follows=True)
            body(c, 2, c * BODIES + 2, False, False, False, False, follows=True)

        @block.sync
        def _(sp):
            sp.dma_start(vec[:, :], vectors).then_inc(vec_in, 16)
            sp.dma_start(q_cond[:, :], cond).then_inc(cond_in, 16)
            sp.dma_start(c_raw.rearrange("p (k n) -> p k n", k=KT),
                         coupling.rearrange("(k p) n -> p k n", p=P)).then_inc(raw_in, 16)
            sp.dma_start(drive[:, 0:T * SW], x_state).then_inc(drive_in, 16)
            sp.dma_start(h128[:, :], hadamard).then_inc(had_in, 16)
            sp.dma_start(ident[:, :], identity).then_inc(ident_in, 16)
            sp.dma_start(wsd_row[:, :], ws_down).then_inc(wsd_in, 16)
            for i, w in enumerate((w_up, w_gate)):
                sp.wait_ge(raw_free, i + 1)
                sp.dma_start(raw[:, :].rearrange("p (k n) -> p k n", k=KT),
                             w.rearrange("(k p) n -> p k n", p=P)).then_inc(raw_in, 16)
            sp.wait_ge(raw_free, 3)
            sp.dma_start(raw[:, :].rearrange("p (k n) -> p k n", k=IT),
                         w_down.rearrange("(k p) n -> p k n", p=P)).then_inc(raw_in, 16)

            def chunk_io(h, first):
                if not first:
                    sp.wait_ge(out_done, 16 * h)
                sp.dma_start(x_res[:, :, :],
                             x_rows[bass.ds(h * RT * P, RT * P), :].rearrange("(a p) n -> p a n", p=P)
                             ).then_inc(x_in, 16)
                sp.wait_ge(y_ready, RT * h + RT)
                sp.dma_start(out[bass.ds(h * RT * P, RT * P), :].rearrange("(a p) n -> p a n", p=P),
                             y_sb[:, :, :]).then_inc(out_done, 16)

            chunk_io(0, True)
            with sp.Fori(1, CHUNKS) as h:
                chunk_io(h, False)
            sp.wait_ge(out_done, 16 * CHUNKS)

        @block.scalar
        def _(act):
            act.wait_ge(ones_set, 2)
            act.activation(warm[:, :], warm[:, :], ACT.Silu).then_inc(table_warm, 1)
            for i, hi in enumerate((wu_hi, wg_hi)):
                act.wait_ge(scale_set, i + 1)
                act.activation(hi[:, :], raw[:, :], ACT.Identity,
                               scale=wscale[:, i:i + 1]).then_inc(w_hi_split, 1)
            act.wait_ge(wsd_spread, 1)
            act.activation(wsd_all[:, :], ps_had[:, :], ACT.Copy).then_inc(wsd_set, 1)
            act.wait_ge(d_scale_set, 1)
            for i in range(IT):
                act.activation(wd_hi[:, i * N:(i + 1) * N], raw[:, i * N:(i + 1) * N], ACT.Identity,
                               scale=dscale[:, i:i + 1]).then_inc(wd_hi_split, 1)

            def q_high(now, at):
                act.wait_ge(rclip_ready, now)
                act.activation(q_parts[:, bass.ds(at, SW)], r_clip[:, :], ACT.Copy,
                               scale=AQ[0] / S).then_inc(qhi_ready, 1)

            def stage(s, now, at):
                i = s % 4
                for x in range(2):
                    act.wait_ge(r_ready[i][x], now)
                    act.activation(t_parts[:, 2 * x:2 * x + 2, 0, :],
                                   half(r[:, i, :], x).rearrange("p (k b) -> p k b", b=B),
                                   ACT.Tanh, scale=AQ[i] / S).then_inc(thi_ready[i][x], 1)
                for x in range(2):
                    act.activation(half(t_full[:, :], x), half(r[:, i, :], x), ACT.Tanh,
                                   scale=AQ[i] / S).then_inc(tfull_ready[i][x], 1)
                c = A[i] * EPSILON
                src = r[:, i, :]
                if i == 0:
                    act.wait_ge(rclip_ready, now)
                    src = r_clip[:, :]
                if i < 3:
                    act.activation(p_drive[:, i, :], src, ACT.Copy,
                                   scale=c * AQ[i]).then_inc(pdrive_ready[i], 1)
                    if i:
                        act.wait_ge(pnext_ready[i], now)
                    else:
                        act.wait_ge(p_ready, now)
                    act.activation(p_decay[:, i, :], p[:, i, :], ACT.Copy,
                                   scale=c * BETA).then_inc(pdecay_ready[i], 1)
                act.activation(p_part[:, i, :], src, ACT.Copy,
                               scale=P_FROM[i] * AQ[i]).then_inc(ppart_ready[i], 1)
                if i == 0:
                    act.activation(p_part[:, 4, :], p[:, 0, :], ACT.Copy,
                                   scale=P_SELF).then_inc(pself_ready, 1)
                if i == 1:
                    act.wait_ge(push_ready[0], now)
                    q_high(now, at)

            def ffn(c, j, n, s, had, gate, down):
                if down and s == 3:
                    act.wait_ge(hid_ready, n - 17)
                    act.wait_ge(down_done, n - 18)
                    act.activation(hid_hi[:, :], hid[:, :], ACT.Copy).then_inc(hidhi_ready, 1)
                if gate and s == 7:
                    act.wait_ge(gate_done, n - 16)
                    act.wait_ge(hid_ready, n - 17)
                    act.activation(sil[:, :], ps_gate[:, 0:ROWS], ACT.Silu,
                                   scale=gscale[:, bass.ds((n - 17) % IT, 1)]).then_inc(sil_ready, 1)
                if had and s in (2, 3):
                    x = s - 2
                    act.wait_ge(had_done, 2 * (c - 1) + x + 1)
                    act.activation(xh_hi_f[:, bass.ds((c - 1) % 2 * (KT * ROWS) + x * 2 * ROWS,
                                                      2 * ROWS)],
                                   ps_had[:, :], ACT.Copy).then_inc(xhi_ready, 1)

            def body(c, j, n, recur, had, gate, down, follows):
                if recur:
                    now = step_counts(act, n)
                    at = [c_ * 2 * SW for c_ in now]
                for s_ in range(SLOTS):
                    if recur:
                        stage(s_, now[s_ // 4], at[s_ // 4])
                    ffn(c, j, n, s_, had, gate, down)

            run_bodies(act, body, lambda: q_high(T + 1, (T + 1) * 2 * SW))

        @block.tensor
        def _(pe):
            pe.wait_ge(ident_in, 16)
            pe.wait_ge(ones_set, 1)
            for i in range(2):
                pe.wait_ge(peaks_found, i + 1)
                pe.transpose(ps_had[0:1, 0:P], peak[:, i:i + 1], ident[:, :]).then_inc(peaks_turned, 1)
                pe.wait_ge(top_found, i + 1)
                pe.matmul(ps_had[:, 0:1], ones[:, :], top[:, 2 * i + 1:2 * i + 2],
                          start=True, stop=True).then_inc(top_spread, 1)
            pe.wait_ge(wsd_in, 16)
            pe.wait_ge(unscale_set, 2)
            pe.matmul(ps_had[:, :], ones[:, :], wsd_row[:, :], start=True, stop=True).then_inc(wsd_spread, 1)
            pe.wait_ge(had_in, 16)
            pe.wait_ge(fly_add, 4)
            pe.wait_ge(fly_sub, 4)
            for i in range(IT):
                if i >= 2:
                    pe.wait_ge(wd_scaled, i - 1)
                pe.matmul([ps_gate, ps_up][i % 2][:, :], h128[:, :], raw[:, i * N:(i + 1) * N],
                          start=True, stop=True).then_inc(wd_rotated, 1)
            pe.wait_ge(wsd_set, 1)
            pe.wait_ge(had_set, 1)
            pe.wait_ge(c_lo_split, 1)
            pe.wait_ge(wd_lo_split, IT)

            def couple(w, x, m, moving, first=False, last=False):
                for a in m:
                    o = (a % 2) * B
                    for kt in (2 * x, 2 * x + 1):
                        done = pe.matmul(
                            prod[a // 2][:, 0:moving, o:o + B], w[:, kt, a * P:(a + 1) * P],
                            t_parts[:, kt, 0:moving, :], start=(first and a % 2 == 0 and kt == 0),
                            stop=(last and a % 2 == 1 and kt == KT - 1), skip_group_check=True)
                return done

            def stage(s, now):
                i = s % 4
                pe.wait_ge(thi_ready[i][0], now)
                couple(c_lo, 0, (0, 1), 1, first=True)
                pe.wait_ge(thi_ready[i][1], now)
                couple(c_lo, 0, (2, 3), 1, first=True)
                couple(c_lo, 1, (0, 1, 2, 3), 1)
                pe.wait_ge(tlo_ready[i][0], now)
                couple(c_hi, 0, (0, 1, 2, 3), 2)
                pe.wait_ge(tlo_ready[i][1], now)
                for h in range(2):
                    couple(c_hi, 1, (2 * h, 2 * h + 1), 2, last=True).then_inc(prod_ready[i][h], 1)

            def rotate(c, x, had_at):
                if x == 0:
                    pe.wait_ge(qlo_ready, c * CHUNK_STEPS + 1)
                    pe.wait_ge(wsd_set, 1)
                if x or not (isinstance(c, int) and c == 1):
                    pe.wait_ge(xlo_ready, 2 * (c - 1) + x)
                base = q_parts[:, bass.ds(had_at, CHUNK_STEPS * 2 * SW)].rearrange(
                    "p (t a k b) -> p t a k b", a=2, k=KT, b=B)
                for o in range(2):
                    for kt in range(KT):
                        sign = bin((2 * x + o) & kt).count("1") % 2
                        for part in range(2):
                            last = pe.matmul(ps_had[:, o * ROWS:(o + 1) * ROWS].rearrange(
                                                 "p (t b) -> p t b", b=B),
                                             (had_m if sign else had_p)[:, kt, :],
                                             base[:, :, part, kt, :],
                                             start=(kt == 0 and part == 0 and o == 0),
                                             stop=(kt == 3 and part == 1 and o == 1),
                                             skip_group_check=True)
                last.then_inc(had_done, 1)

            def ffn(c, j, n, s, recur, had, gate, down, tile, rows_at, down_tile, had_at):
                if had and s == 2:
                    rotate(c, 0, had_at)
                if gate:
                    for m in range(sum(GU_SHARE[:s]), sum(GU_SHARE[:s + 1])):
                        side, kt, x = m // 12, m // 3 % 4, m % 3
                        a, b = ((0, 0), (1, 0), (0, 1))[x]
                        w = ((wg_hi, wg_lo), (wu_hi, wu_lo))[side][a]
                        bank, ready = ((ps_gate, gate_done), (ps_up, up_done))[side]
                        xs = (xh_hi_f, xh_lo_f)[b]
                        if m == 0 and not recur:
                            pe.wait_ge(sil_ready, n - 17)
                        if m == 12 and not recur:
                            pe.wait_ge(hid_ready, n - 17)
                        if isinstance(j, int) and j == 1 and m in (0, 6):
                            pe.wait_ge(xhi_ready, 2 * (c - 1) + 1 + m // 6)
                            pe.wait_ge(xlo_ready, 2 * (c - 1) + 1 + m // 6)
                        last = pe.matmul(bank[:, 0:ROWS],
                                         w[:, kt * INTER:(kt + 1) * INTER][:, bass.ds(tile, P)],
                                         xs[:, bass.ds(rows_at + kt * ROWS, ROWS)],
                                         start=(kt == 0 and x == 0), stop=(kt == 3 and x == 2))
                        if m % 12 == 11:
                            last.then_inc(ready, 1)
                for m in range(6):
                    if not down or DOWN_SLOTS[m] != s:
                        continue
                    a, x = m // 3, m % 3
                    if x == 0:
                        pe.wait_ge(hidlo_ready, 2 * (n - 18) + a + 1)
                    first = isinstance(j, int) and j == 2
                    end = isinstance(j, int) and j == 1
                    if first and x == 0 and not (isinstance(c, int) and c == 1):
                        pe.wait_ge(y_ready, RT * (c - 2) + a + 1)
                    last = pe.matmul(ps_y[a][:, :], (hid_hi, hid_hi, hid_lo)[x][:, a * P:(a + 1) * P],
                                     (wd_hi, wd_lo, wd_hi)[x][:, bass.ds(down_tile, N)],
                                     start=(first and x == 0), stop=(end and x == 2),
                                     skip_group_check=True)
                    if m == 5:
                        last.then_inc(down_done, 1)
                if had and s == 2:
                    rotate(c, 1, had_at)

            def keep_clock():
                pe.matmul(ps_had[:, 0:2 * P], had_p[:, 0, :],
                          had_p[:, 0:2, :].rearrange("p k n -> p (k n)"), start=True, stop=True)

            def body(c, j, n, recur, had, gate, down, follows):
                fixed = isinstance(n, int)
                hold = (lambda v: v) if fixed else pe.snap
                now = step_counts(pe, n) if recur else None
                tile = hold((n - 17) % IT * P) if gate else None
                rows_at = hold((n - 17) // BODIES % 2 * (KT * ROWS)) if gate else None
                down_tile = hold((n - 18) % IT * N) if down else None
                had_at = ((c - 1) * CHUNK_STEPS + 2) * 2 * SW if had else None
                if had and not isinstance(c, int):
                    had_at = pe.snap(had_at)
                for s_ in range(SLOTS):
                    if recur:
                        stage(s_, now[s_ // 4])
                    ffn(c, j, n, s_, recur, had, gate, down, tile, rows_at, down_tile, had_at)
                    if recur and gate and s_ in FILL_SLOTS and not (had and s_ == 3):
                        keep_clock()

            run_bodies(pe, body)

        @block.vector
        def _(dve):
            dve.memset(ones[:, :], 1.0).then_inc(ones_set, 1)
            dve.memset(warm[:, :], 0.0).then_inc(ones_set, 1)
            dve.wait_ge(raw_in, 16)
            c_hi_f, c_lo_f = [c[:, :, :].rearrange("p k n -> p (k n)") for c in (c_hi, c_lo)]
            dve.tensor_scalar(c_hi_f, c_raw, S, None, ALU.mult).then_inc(c_hi_split, 1)
            dve.wait_ge(c_hi_split, 1)
            dve.scalar_tensor_tensor(out=c_lo_f, in0=c_raw, scalar=S, in1=c_hi_f, op0=ALU.mult,
                                     op1=ALU.subtract).then_inc(c_lo_split, 1)
            dve.wait_ge(c_lo_split, 1)
            dve.memset(rec[:, 0:1], 0.0).then_inc(raw_free, 1)
            dve.wait_ge(vec_in, 16)
            dve.wait_ge(drive_in, 16)
            dve.tensor_scalar(bias[:, :], vec[:, V_BIAS:V_BIAS + KT], P_SHIFT, None,
                              ALU.subtract).then_inc(bias_set, 1)
            dve.wait_ge(bias_set, 1)
            drive_v = drive[:, 0:T * SW].rearrange("p (t k b) -> p t k b", k=KT, b=B)
            for kt in range(KT):
                dve.tensor_scalar(drive_v[:, :, kt, :], drive_v[:, :, kt, :],
                                  bias[:, kt:kt + 1], S, ALU.add,
                                  ALU.mult).then_inc(drive_set, 1)
            dve.wait_ge(had_in, 16)
            for kt in range(KT):
                sign = vec[:, V_SUUG + kt:V_SUUG + kt + 1]
                dve.tensor_scalar(had_p[:, kt, :], h128[:, :], sign, None, ALU.mult)
                last = dve.tensor_scalar(had_m[:, kt, :], h128[:, :], sign, -1.0, ALU.mult, ALU.mult)
            last.then_inc(had_set, 1)
            for i, (hi, lo) in enumerate(((wu_hi, wu_lo), (wg_hi, wg_lo))):
                dve.wait_ge(raw_in, 32 + 16 * i)
                dve.tensor_reduce(peak[:, i:i + 1], raw[:, :], AX.X, ALU.max,
                                  apply_absolute_value=True).then_inc(peaks_found, 1)
                dve.wait_ge(peaks_turned, i + 1)
                dve.tensor_reduce(top[:, 2 * i:2 * i + 1], ps_had[0:1, 0:P], AX.X,
                                  ALU.max).then_inc(scales_step, 1)
                dve.wait_ge(scales_step, 2 * i + 1)
                dve.tensor_scalar(top[:, 2 * i + 1:2 * i + 2], top[:, 2 * i:2 * i + 1],
                                  1.0 / FP16_TOP, 1e-30, ALU.mult, ALU.max).then_inc(top_found, 1)
                dve.wait_ge(top_spread, i + 1)
                dve.tensor_copy(unscale[:, i:i + 1], ps_had[:, 0:1]).then_inc(unscale_set, 1)
                dve.wait_ge(unscale_set, i + 1)
                dve.reciprocal(wscale[:, i:i + 1], unscale[:, i:i + 1]).then_inc(scale_set, 1)
                dve.wait_ge(w_hi_split, i + 1)
                dve.scalar_tensor_tensor(out=lo[:, :], in0=raw[:, :], scalar=wscale[:, i:i + 1],
                                         in1=hi[:, :], op0=ALU.mult,
                                         op1=ALU.subtract).then_inc(w_lo_split, 1)
                dve.wait_ge(w_lo_split, i + 1)
                dve.memset(top[:, 2 * i:2 * i + 1], 0.0).then_inc(raw_free, 1)
                dve.wait_ge(raw_free, i + 2)
                dve.memset(utmp[:, :, :], 0.0).then_inc(scales_step, 1)
            dve.wait_ge(raw_in, 64)
            for lv in range(4):
                src, dst = (raw, wd_buf) if lv % 2 == 0 else (wd_buf, raw)
                w = (1 << lv) * N
                sv = src[:, :].rearrange("p (g a w) -> p g a w", a=2, w=w)
                dv = dst[:, :].rearrange("p (g a w) -> p g a w", a=2, w=w)
                if lv:
                    dve.wait_ge(fly_add, lv)
                    dve.wait_ge(fly_sub, lv)
                dve.tensor_tensor(dv[:, :, 0, :], sv[:, :, 0, :], sv[:, :, 1, :],
                                  ALU.add).then_inc(fly_add, 1)
            dve.wait_ge(wsd_set, 1)
            for i in range(IT):
                dve.wait_ge(wd_rotated, i + 1)
                dve.tensor_tensor(raw[:, i * N:(i + 1) * N], [ps_gate, ps_up][i % 2][:, :],
                                  wsd_all[:, :], ALU.mult).then_inc(wd_scaled, 1)
            dve.wait_ge(wd_scaled, IT)
            dve.tensor_reduce(dpeak[:, :], raw[:, :].rearrange("p (i n) -> p i n", n=N), AX.X,
                              ALU.max, apply_absolute_value=True).then_inc(scales_step, 1)
            dve.wait_ge(scales_step, 5)
            dve.tensor_scalar(dunscale[:, :], dpeak[:, :], 1.0 / FP16_TOP, 1e-30, ALU.mult,
                              ALU.max).then_inc(d_unscale_set, 1)
            dve.wait_ge(d_unscale_set, 1)
            dve.reciprocal(dscale[:, :], dunscale[:, :]).then_inc(d_scale_set, 1)
            root = float(N) ** -0.5
            dve.tensor_scalar(gscale[:, :], vec[:, V_WGATE:V_WGATE + IT], unscale[:, 1:2], root,
                              ALU.mult, ALU.mult)
            dve.tensor_scalar(utmp[:, 0, :], vec[:, V_WUP:V_WUP + IT], unscale[:, 0:1],
                              root * float(INTER) ** -0.5, ALU.mult, ALU.mult).then_inc(scales_step, 1)
            dve.wait_ge(scales_step, 6)
            dve.tensor_tensor(utmp[:, 1, :], utmp[:, 0, :], vec[:, V_SUDP:V_SUDP + IT],
                              ALU.mult).then_inc(scales_step, 1)
            dve.wait_ge(scales_step, 7)
            dve.tensor_tensor(uscale[:, :], utmp[:, 1, :], dunscale[:, :],
                              ALU.mult).then_inc(scales_step, 1)
            for i in range(IT):
                dve.wait_ge(wd_hi_split, i + 1)
                dve.scalar_tensor_tensor(out=wd_lo[:, i * N:(i + 1) * N],
                                         in0=raw[:, i * N:(i + 1) * N], scalar=dscale[:, i:i + 1],
                                         in1=wd_hi[:, i * N:(i + 1) * N], op0=ALU.mult,
                                         op1=ALU.subtract).then_inc(wd_lo_split, 1)
            dve.wait_ge(cond_in, 16)
            dve.wait_ge(scales_step, 8)
            for x in range(2):
                dve.tensor_scalar(half(r[:, 0, :], x), half(q_cond[:, :], x), S / AQ[0], None,
                                  ALU.mult).then_inc(r_ready[0][x], 1)

            def t_low(i, x, now):
                dve.wait_ge(tfull_ready[i][x], now)
                dve.tensor_tensor(t_parts[:, 2 * x:2 * x + 2, 1, :],
                                  half(t_full[:, :], x).rearrange("p (k b) -> p k b", b=B),
                                  t_parts[:, 2 * x:2 * x + 2, 0, :],
                                  ALU.subtract).then_inc(tlo_ready[i][x], 1)

            def clip(now, first):
                bound = CLAMP * S / AQ[0]
                dve.wait_ge(r_ready[0][1], now)
                if first:
                    step = dve.tensor_scalar(r_clip[:, :], r[:, 0, :], 1.0, None, ALU.mult)
                else:
                    step = dve.tensor_scalar(r_clip[:, :], r[:, 0, :], bound, -bound, ALU.min,
                                             ALU.max)
                step.then_inc(rclip_ready, 1)

            def q_low(now, at):
                dve.wait_ge(qhi_ready, now)
                dve.scalar_tensor_tensor(out=q_parts[:, bass.ds(at + SW, SW)], in0=r_clip[:, :],
                                         scalar=AQ[0] / S, in1=q_parts[:, bass.ds(at, SW)],
                                         op0=ALU.mult, op1=ALU.subtract).then_inc(qlo_ready, 1)

            def stage(s, now, at, first):
                i = s % 4
                src = r_clip[:, :] if i == 0 else r[:, i, :]

                def square():
                    if i:
                        dve.wait_ge(r_ready[i][1], now)
                    else:
                        dve.wait_ge(rclip_ready, now)
                    dve.scalar_tensor_tensor(out=q_sq[:, i, :], in0=src,
                                             scalar=-(AQ[i] / S) ** 2 / 3, in1=src, op0=ALU.mult,
                                             op1=ALU.mult).then_inc(sq_ready[i], 1)

                def cubic():
                    dve.wait_ge(sq_ready[i], now)
                    dve.scalar_tensor_tensor(out=fq[:, i, :], in0=q_sq[:, i, :], scalar=1.0,
                                             in1=src, op0=ALU.add, op1=ALU.mult).then_inc(fq_ready[i], 1)

                def rest():
                    if i < 3:
                        dve.wait_ge(push_ready[i], now)
                        in0, scale, in1 = r_clip[:, :], BASE[i], push[:, i, :]
                    else:
                        dve.wait_ge(accpush_ready, now)
                        in0, scale, in1 = r[:, 3, :], 2.0, acc_push[:, :]
                    dve.scalar_tensor_tensor(out=base_push[:, i, :], in0=in0, scalar=scale, in1=in1,
                                             op0=ALU.mult, op1=ALU.add).then_inc(bpush_ready[i], 1)

                if i == 0:
                    clip(now, first)
                    square()
                    t_low(i, 0, now)
                    cubic()
                    t_low(i, 1, now)
                    rest()
                elif i < 3:
                    square()
                    rest()
                    cubic()
                    t_low(i, 0, now)
                    t_low(i, 1, now)
                else:
                    square()
                    cubic()
                    t_low(i, 0, now)
                    t_low(i, 1, now)
                    rest()
                dve.wait_ge(bpush_ready[i], now)
                dve.wait_ge(fq_ready[i], now)
                dve.scalar_tensor_tensor(out=b_full, in0=halves(fq[:, i, :]), scalar=AQ[i],
                                         in1=halves(base_push[:, i, :]), op0=ALU.mult,
                                         op1=ALU.add).then_inc(bfull_ready[i], 1)
                if i == 1:
                    dve.scalar_tensor_tensor(out=r_acc[:, 0, :], in0=r_clip[:, :], scalar=-BASE_EXCESS,
                                             in1=r[:, 1, :], op0=ALU.mult,
                                             op1=ALU.add).then_inc(acc1_ready, 1)
                if i == 2:
                    dve.wait_ge(acc1_ready, now)
                    dve.scalar_tensor_tensor(out=r_acc[:, 1, :], in0=r[:, 2, :], scalar=2.0,
                                             in1=r_acc[:, 0, :], op0=ALU.mult,
                                             op1=ALU.add).then_inc(acc2_ready, 1)
                    q_low(now, at)

            def next_r(s, now):
                i = s % 4
                for x in range(2):
                    dve.wait_ge(prod_ready[i][x], now)
                    if x == 0:
                        dve.wait_ge(bfull_ready[i], now)
                    dve.tensor_reduce(half(r[:, (i + 1) % 4, :], x), sum_full[x], AX.X,
                                      ALU.add).then_inc(r_ready[(i + 1) % 4][x], 1)

            def rotated_low(c, x):
                at = (c - 1) % 2 * (KT * ROWS) + x * 2 * ROWS
                dve.wait_ge(xhi_ready, 2 * (c - 1) + x + 1)
                dve.tensor_tensor(xh_lo_f[:, bass.ds(at, 2 * ROWS)], ps_had[:, :],
                                  xh_hi_f[:, bass.ds(at, 2 * ROWS)],
                                  ALU.subtract).then_inc(xlo_ready, 1)

            def hidden(n, recur):
                if not recur:
                    dve.wait_ge(hidlo_ready, 2 * (n - 18))
                    dve.wait_ge(sil_ready, n - 17)
                    dve.wait_ge(up_done, n - 17)
                dve.scalar_tensor_tensor(out=hid[:, :], in0=ps_up[:, 0:ROWS],
                                         scalar=uscale[:, bass.ds((n - 18) % IT, 1)], in1=sil[:, :],
                                         op0=ALU.mult, op1=ALU.mult).then_inc(hid_ready, 1)

            def output(c, a):
                dve.wait_ge(down_done, (c - 1) * BODIES)
                dve.wait_ge(x_in, 16 * (c - 1))
                dve.tensor_tensor(y_sb[:, a, :], ps_y[a][:, :], x_res[:, a, :],
                                  ALU.add).then_inc(y_ready, 1)

            next_step = []

            def body(c, j, n, recur, had, gate, down, follows):
                hold = (lambda v: v) if isinstance(n, int) else dve.snap
                first = isinstance(n, int) and n == 0
                if recur:
                    now = next_step.pop() if follows else hold(n * BODY_STEPS + 1)
                    next_step.clear()
                for s_ in range(SLOTS):
                    if recur:
                        if s_ == 4:
                            now = after
                        stage(s_, now, at if s_ % 4 == 2 else None, first and s_ == 0)
                    if recur and s_ % 4 == 1:
                        at = hold(now * (2 * SW))
                    if recur and s_ == 2:
                        after = hold(now + 1)
                    if recur and s_ == 6:
                        next_step.append(hold(now + 1))
                    if had and s_ == 3:
                        rotated_low(c, 1)
                    if down and s_ == 1:
                        hidden(n, recur)
                    if (isinstance(j, int) and j == 2 and s_ in (2, 5)
                            and not (isinstance(c, int) and c == 1)):
                        output(c, s_ // 3)
                    if recur:
                        next_r(s_, now)
                    if had and s_ == 2:
                        rotated_low(c, 0)

            def last_q():
                clip(T + 1, False)
                q_low(T + 1, (T + 1) * 2 * SW)

            run_bodies(dve, body, last_q, group=3)

        @block.gpsimd
        def _(pool):
            pool.wait_ge(cond_in, 16)
            pool.tensor_scalar(p[:, 0, :], q_cond[:, :], S, -S * P_SHIFT, ALU.mult,
                               ALU.add).then_inc(p_ready, 1)
            pool.wait_ge(raw_in, 64)
            for lv in range(4):
                src, dst = (raw, wd_buf) if lv % 2 == 0 else (wd_buf, raw)
                w = (1 << lv) * N
                sv = src[:, :].rearrange("p (g a w) -> p g a w", a=2, w=w)
                dv = dst[:, :].rearrange("p (g a w) -> p g a w", a=2, w=w)
                if lv:
                    pool.wait_ge(fly_add, lv)
                    pool.wait_ge(fly_sub, lv)
                pool.tensor_tensor(dv[:, :, 1, :], sv[:, :, 0, :], sv[:, :, 1, :],
                                   ALU.subtract).then_inc(fly_sub, 1)
            pool.wait_ge(drive_set, KT)

            def wait_apart(signal, count):
                count = pool.snap(count) if not isinstance(count, int) else count
                pool.wait_ge(cond_in, 16)
                pool.wait_ge(signal, count)

            def stage(s, now, at):
                i = s % 4
                if i == 0:
                    pool.wait_ge(p_ready, now)
                    pool.tensor_tensor(push[:, 0, :], track[:, bass.ds(at, SW)], p[:, 0, :],
                                       ALU.subtract).then_inc(push_ready[0], 1)
                if i < 3:
                    pool.wait_ge(pdrive_ready[i], now)
                    pool.wait_ge(pdecay_ready[i], now)
                    pool.tensor_tensor(p_move[:, i, :], p_drive[:, i, :], p_decay[:, i, :],
                                       ALU.subtract).then_inc(pmove_ready[i], 1)
                    pool.wait_ge(pmove_ready[i], now)
                    pool.tensor_tensor(push[:, i + 1, :], push[:, 0, :], p_move[:, i, :],
                                       ALU.subtract).then_inc(push_ready[i + 1], 1)
                if i < 2:
                    pool.tensor_tensor(p[:, i + 1, :], p[:, 0, :], p_move[:, i, :],
                                       ALU.add).then_inc(pnext_ready[i + 1], 1)
                if i == 2:
                    pool.wait_ge(push_ready[3], now)
                    pool.wait_ge(acc2_ready, now)
                    pool.tensor_tensor(acc_push[:, :], r_acc[:, 1, :], push[:, 3, :],
                                       ALU.add).then_inc(accpush_ready, 1)
                if i < 3:
                    pool.wait_ge(ppart_ready[i], now)
                    if i == 0:
                        pool.wait_ge(pself_ready, now)
                    else:
                        pool.wait_ge(pacc_ready[i - 1], now)
                    pool.tensor_tensor(p_acc[:, i, :], p_part[:, 4, :] if i == 0 else p_acc[:, i - 1, :],
                                       p_part[:, i, :], ALU.add).then_inc(pacc_ready[i], 1)
                if i == 3:
                    pool.wait_ge(pacc_ready[2], now)
                    pool.tensor_tensor(p_acc[:, 3, :], p[:, 0, :], p_acc[:, 2, :],
                                       ALU.add).then_inc(pacc_ready[3], 1)
                    pool.wait_ge(ppart_ready[3], now)
                    pool.wait_ge(pacc_ready[3], now)
                    pool.tensor_tensor(p_raw[:, :], p_acc[:, 3, :], p_part[:, 3, :],
                                       ALU.add).then_inc(praw_ready, 1)
                    wait_apart(praw_ready, now)
                    pool.tensor_scalar(p[:, 0, :], p_raw[:, :], (CLAMP - P_SHIFT) * S,
                                       (-CLAMP - P_SHIFT) * S, ALU.min, ALU.max).then_inc(p_ready, 1)

            def ffn(c, j, n, s, had, gate, down):
                if down and s in (5, 6):
                    a = s - 5
                    rows = slice(a * P, (a + 1) * P)
                    pool.wait_ge(hidhi_ready, n - 17)
                    pool.tensor_tensor(hid_lo[:, rows], hid[:, rows], hid_hi[:, rows],
                                       ALU.subtract).then_inc(hidlo_ready, 1)

            def body(c, j, n, recur, had, gate, down, follows):
                if recur:
                    now = step_counts(pool, n)
                    at = [c_ * SW for c_ in now]
                for s_ in range(SLOTS):
                    ffn(c, j, n, s_, had, gate, down)
                    if recur:
                        stage(s_, now[s_ // 4], at[s_ // 4])

            run_bodies(pool, body)


def _hadamard():
    h = np.ones((1, 1), np.float32)
    while h.shape[0] < P:
        h = np.block([[h, h], [h, -h]])
    return np.ascontiguousarray(h.astype(np.float32))


def kernel(x, cond_2048, L0_cond_coupling, L0_cond_bias, L0_ffn_SU_ug, L0_ffn_SU_dp,
           L0_ffn_Wscale_ug, L0_ffn_Wscale_dp, L0_ffn_W_up, L0_ffn_W_gate, L0_ffn_W_down):
    import concourse.bacc as bacc
    from concourse.bass_utils import run_bass_kernel_spmd

    def columns(v):
        return np.asarray(v).reshape(-1, P).T

    x = np.asarray(x)
    arrays = {
        "x_state": x.reshape(B, T, KT, P).transpose(3, 1, 2, 0).reshape(P, T * SW),
        "x_rows": x.transpose(1, 0, 2).reshape(T * B, N),
        "cond": np.asarray(cond_2048).reshape(B, KT, P).transpose(2, 1, 0).reshape(P, SW),
        "coupling": np.asarray(L0_cond_coupling).T,
        "w_up": np.asarray(L0_ffn_W_up).T,
        "w_gate": np.asarray(L0_ffn_W_gate).T,
        "w_down": np.asarray(L0_ffn_W_down).T,
        "vectors": np.concatenate([columns(L0_cond_bias), columns(L0_ffn_SU_ug),
                                   columns(L0_ffn_Wscale_ug), columns(L0_ffn_SU_dp)], axis=1),
        "ws_down": np.asarray(L0_ffn_Wscale_dp).reshape(1, N),
        "hadamard": _hadamard(),
        "identity": np.eye(P, dtype=np.float32),
    }
    arrays = {n: np.ascontiguousarray(a) for n, a in arrays.items()}
    nc = bacc.Bacc("TRN2", target_bir_lowering=False, num_devices=1)
    args = {n: nc.dram_tensor("in_" + n, a.shape, mybir.dt.from_np(a.dtype), kind="ExternalInput").ap()
            for n, a in arrays.items()}
    out = nc.dram_tensor("out_rows", (T * B, N), F32, kind="ExternalOutput").ap()
    build(nc, out=out, **args)
    res = run_bass_kernel_spmd(nc, [{"in_" + n: a for n, a in arrays.items()}], core_ids=[0])
    rows = res.results[0]["out_rows"]
    return np.ascontiguousarray(rows.reshape(T, B, N).transpose(1, 0, 2))
```

```python
from contextlib import ExitStack

import numpy as np

import concourse.bass as bass
from concourse import mybir

F32 = mybir.dt.float32
F16 = mybir.dt.float16
BF16 = mybir.dt.bfloat16
ALU = mybir.AluOpType
ACT = mybir.ActivationFunctionType
AX = mybir.AxisListType

P = 128
B = 8
T = 256
N = 512
INTER = 2048
KT = N // P
IT = INTER // P
SW = KT * B
HW = SW // 2

DT = 0.01
EPSILON = 0.08
ALPHA = 0.7
BETA = 0.8
CLAMP = 20.0
S = 64.0
A = [DT / 2, DT / 2, DT, DT / 6]
P_SHIFT = ALPHA / BETA
_E, _Z = EPSILON * DT, EPSILON * BETA * DT
P_SELF = -_Z + _Z ** 2 / 2 - _Z ** 3 / 6 + _Z ** 4 / 24
P_FROM = [_E / 6 * (1 - _Z + _Z ** 2 / 2 - _Z ** 3 / 4), _E / 6 * (2 - _Z + _Z ** 2 / 2),
          _E / 6 * (2 - _Z), _E / 6]
AQ = [A[3], A[0], A[1], A[2]]
BASE = [float(np.float32(AQ[0] / a)) for a in A[:3]]
BASE_EXCESS = BASE[0] + 2 * BASE[1] + 2 * BASE[2] - 1
assert float(np.float32(BASE_EXCESS)) == BASE_EXCESS

BODY_STEPS = 2
SLOTS = 4 * BODY_STEPS
ROWS = 256
RT = ROWS // P
CHUNK_STEPS = ROWS // B
CHUNKS = T // CHUNK_STEPS
BODIES = CHUNK_STEPS // BODY_STEPS
assert BODIES == IT
DOWN_SLOTS = [5, 5, 6, 6, 7, 7]
GU_SHARE = [5, 5, 5, 4, 5, 0, 0, 0]
GU_SHARE_HAD = [5, 5, 2, 0, 4, 3, 3, 2]
FILL = [0, 0, 0, 1, 0, 1, 1, 1]
FILL_HAD = [0, 0, 0, 4, 2, 0, 0, 0]
assert sum(GU_SHARE) == sum(GU_SHARE_HAD) == 2 * 3 * KT
FP16_TOP = 1024.0

V_BIAS, V_SUUG, V_WUP, V_WGATE, V_SUDP, V_COLS = 0, 4, 8, 24, 40, 56


def build(nc, x_state, x_rows, cond, coupling, w_up, w_gate, w_down, vectors, ws_down, hadamard,
          identity, out):
    with ExitStack() as ctx:
        def sb(name, shape, dt=F32):
            return ctx.enter_context(nc.sbuf_tensor(name, shape, dt))

        def sem(name):
            return ctx.enter_context(nc.semaphore(name))

        raw = sb("raw", [P, IT * N])
        c_raw = raw[:, 0:KT * N]
        c_hi = sb("c_hi", [P, KT, N], F16)
        c_lo = sb("c_lo", [P, KT, N], F16)
        wu_hi = sb("wu_hi", [P, KT * INTER], F16)
        wu_lo = sb("wu_lo", [P, KT * INTER], F16)
        wg_hi = sb("wg_hi", [P, KT * INTER], F16)
        wg_lo = sb("wg_lo", [P, KT * INTER], F16)
        wd_buf = sb("wd_buf", [P, IT * N])
        wd_parts = wd_buf[:, :].bitcast(F16)
        wd_hi = wd_parts[:, 0:IT * N]
        wd_lo = wd_parts[:, IT * N:2 * IT * N]
        vec = sb("vec", [P, V_COLS])
        h128 = sb("h128", [P, P])
        ident = sb("ident", [P, P])
        ones = sb("ones", [1, P])
        wsd_row = sb("wsd_row", [1, N])
        wsd_all = sb("wsd_all", [P, N])
        had_p = sb("had_p", [P, KT, P], F16)
        had_m = sb("had_m", [P, KT, P], F16)
        peak = sb("peak", [P, 2])
        top = sb("top", [1, 4])
        unscale = sb("unscale", [P, 2])
        wscale = sb("wscale", [P, 2])
        dpeak = sb("dpeak", [P, IT])
        dunscale = sb("dunscale", [P, IT])
        dscale = sb("dscale", [P, IT])
        gscale = sb("gscale", [P, IT])
        uscale = sb("uscale", [P, IT])
        utmp = sb("utmp", [P, 2, IT])
        warm = sb("warm", [P, 1])
        bias = sb("bias", [P, KT])

        track = sb("track", [P, (T + 2) * SW])
        drive = track[:, SW:]
        gu_raw = [track[:, 0:KT * INTER], wd_buf[:, 0:KT * INTER]]
        q_parts = track[:, :].bitcast(F16)
        t_parts = sb("t_parts", [P, KT, 2, B], F16)
        t_full = sb("t_full", [P, SW])
        r = sb("r", [P, 4, SW])
        r_clip = sb("r_clip", [P, SW])
        q_cond = sb("q_cond", [P, SW])
        q_sq = sb("q_sq", [P, 4, SW])
        fq = sb("fq", [P, 4, SW])
        base_push = sb("base_push", [P, 4, SW])
        r_acc = sb("r_acc", [P, 2, SW])
        acc_push = sb("acc_push", [P, SW])
        p = sb("p", [P, 3, SW])
        p_raw = sb("p_raw", [P, SW])
        p_decay = sb("p_decay", [P, 3, SW])
        p_drive = sb("p_drive", [P, 3, SW])
        p_move = sb("p_move", [P, 3, SW])
        p_part = sb("p_part", [P, 5, SW])
        p_acc = sb("p_acc", [P, 4, SW])
        push = sb("push", [P, 4, SW])

        xh_hi = sb("xh_hi", [P, 2, KT * ROWS], F16)
        xh_lo = sb("xh_lo", [P, 2, KT * ROWS], F16)
        xh_hi_f = xh_hi[:, :, :].rearrange("p a b -> p (a b)")
        xh_lo_f = xh_lo[:, :, :].rearrange("p a b -> p (a b)")
        sil = sb("sil", [P, ROWS])
        hid = sb("hid", [P, ROWS])
        hid_hi = sb("hid_hi", [P, ROWS], BF16)
        hid_lo = sb("hid_lo", [P, ROWS], BF16)
        x_res = sb("x_res", [P, RT, N])
        y_sb = sb("y_sb", [P, RT, N])

        rec = ctx.enter_context(nc.psum_tensor("rec", [P, 3 * 512], F32))
        prod = [rec[:, o:o + 512].rearrange("p (s c) -> p s c", s=2) for o in (0, 1024)]
        sum_full = [rec[:, o:o + 768].rearrange("p (s c) -> p c s", s=3)[:, 0:HW, :]
                    for o in (0, 768)]
        b_full = rec[:, 512:1024].rearrange("p (h c) -> p h c", h=2)[:, :, 0:HW]

        def halves(ap):
            return ap.rearrange("p (h c) -> p h c", h=2)

        def half(ap, x):
            return ap[:, x * HW:(x + 1) * HW]

        ps_gate, ps_up, ps_had, ps_y0, ps_y1 = [
            ctx.enter_context(nc.psum_tensor(n, [P, 512], F32))
            for n in ("ps_gate", "ps_up", "ps_had", "ps_y0", "ps_y1")]
        ps_y = [ps_y0, ps_y1]
        ps_rot = [ps_had, ps_up]

        vec_in, had_in, ident_in, cond_in, drive_in, wsd_in = [
            sem(n) for n in ("vec_in", "had_in", "ident_in", "cond_in", "drive_in", "wsd_in")]
        c_in, gu_in, down_in, peaks_found, peaks_turned, top_found, top_spread, scale_set, \
            unscale_set, w_hi_split, w_lo_split = [
                sem(n) for n in ("c_in", "gu_in", "down_in", "peaks_found", "peaks_turned", "top_found",
                                 "top_spread", "scale_set", "unscale_set", "w_hi_split",
                                 "w_lo_split")]
        gu_in = [gu_in, sem("gate_in")]
        fly_add, fly_sub, wd_rotated, wd_scaled, d_unscale_set, d_scale_set, wd_hi_split, \
            wd_lo_split = [
                sem(n) for n in ("fly_add", "fly_sub", "wd_rotated", "wd_scaled", "d_unscale_set",
                                 "d_scale_set", "wd_hi_split", "wd_lo_split")]
        c_hi_split, c_lo_split, ones_set, wsd_spread, wsd_set, had_set, drive_set, scales_step, \
            table_warm, bias_set = [
                sem(n) for n in ("c_hi_split", "c_lo_split", "ones_set", "wsd_spread", "wsd_set",
                                 "had_set", "drive_set", "scales_step", "table_warm",
                                 "bias_set")]
        def sem_set(name, *shape):
            if not shape:
                return sem(name)
            return [sem_set(f"{name}_{i}", *shape[1:]) for i in range(shape[0])]

        r_ready, thi_ready, tfull_ready, tlo_ready, prod_ready = [
            sem_set(n, 4, 2) for n in ("r_ready", "thi_ready", "tfull_ready", "tlo_ready",
                                       "prod_ready")]
        sq_ready, fq_ready, bpush_ready, bfull_ready, ppart_ready, pacc_ready, push_ready = [
            sem_set(n, 4) for n in ("sq_ready", "fq_ready", "bpush_ready", "bfull_ready",
                                    "ppart_ready", "pacc_ready", "push_ready")]
        pdecay_ready, pdrive_ready, pmove_ready, pnext_ready = [
            sem_set(n, 3) for n in ("pdecay_ready", "pdrive_ready", "pmove_ready", "pnext_ready")]
        rclip_ready, acc1_ready, acc2_ready, accpush_ready, pself_ready, praw_ready, p_ready, \
            qhi_ready, qlo_ready = [
                sem(n) for n in ("rclip_ready", "acc1_ready", "acc2_ready", "accpush_ready",
                                 "pself_ready", "praw_ready", "p_ready", "qhi_ready",
                                 "qlo_ready")]
        had_done, xhi_ready, xlo_ready, y_ready, x_in, out_done = [
            sem(n) for n in ("had_done", "xhi_ready", "xlo_ready", "y_ready", "x_in", "out_done")]
        gate_done, up_done, sil_ready, hid_ready, hidhi_ready, hidlo_ready, down_done = [
            sem(n) for n in ("gate_done", "up_done", "sil_ready", "hid_ready",
                             "hidhi_ready", "hidlo_ready", "down_done")]

        def butterfly(lv):
            src, dst = (raw, wd_buf) if lv % 2 == 0 else (wd_buf, raw)
            sv, dv = [v[:, :].rearrange("p (g a w) -> p g a w", a=2, w=(1 << lv) * N)
                      for v in (src, dst)]
            return dv[:, :, 0, :], dv[:, :, 1, :], sv[:, :, 0, :], sv[:, :, 1, :]

        block = ctx.enter_context(nc.Block())

        def step_counts(eng, n):
            counts = [n * BODY_STEPS + k + 1 for k in range(BODY_STEPS)]
            return counts if isinstance(n, int) else [eng.snap(c) for c in counts]

        def run_bodies(eng, body, idle=None, group=1, first_group=1):
            lead = 3 if group == 1 else 4

            def chunk(c, recur):
                one = isinstance(c, int) and c == 1
                body(c, 0, c * BODIES, recur, True, not one, not one, follows=False)
                body(c, 1, c * BODIES + 1, recur, False, True, not one, follows=True)
                for j in range(2, lead):
                    body(c, j, c * BODIES + j, recur, False, True, True, follows=True)
                with eng.Fori(0, (BODIES - lead) // group) as turn:
                    for k in range(group):
                        j = turn * group + (lead + k)
                        body(c, j, c * BODIES + j, recur, False, True, True, follows=k > 0)

            first = 0
            if group > 1:
                first = 1
                body(0, None, 0, True, False, False, False, follows=False)
            assert (BODIES - first) % first_group == 0 and (BODIES - lead) % group == 0
            with eng.Fori(0, (BODIES - first) // first_group) as turn:
                for k in range(first_group):
                    body(0, None, turn * first_group + (first + k), True, False, False, False, follows=k > 0)
            chunk(1, True)
            with eng.Fori(2, CHUNKS) as c:
                chunk(c, True)
            if idle:
                idle()
            chunk(CHUNKS, False)
            c = CHUNKS + 1
            body(c, 0, c * BODIES, False, False, True, True, follows=False)
            body(c, 1, c * BODIES + 1, False, False, False, True, follows=True)
            body(c, 2, c * BODIES + 2, False, False, False, False, follows=True)

        @block.sync
        def _(sp):
            sp.dma_start(vec[:, :], vectors).then_inc(vec_in, 16)
            sp.dma_start(q_cond[:, :], cond).then_inc(cond_in, 16)
            sp.dma_start(c_raw.rearrange("p (k n) -> p k n", k=KT),
                         coupling.rearrange("(k p) n -> p k n", p=P)).then_inc(c_in, 16)
            sp.dma_start(gu_raw[0].rearrange("p (k n) -> p k n", k=KT),
                         w_up.rearrange("(k p) n -> p k n", p=P)).then_inc(gu_in[0], 16)
            sp.dma_start(h128[:, :], hadamard).then_inc(had_in, 16)
            sp.dma_start(ident[:, :], identity).then_inc(ident_in, 16)
            sp.dma_start(wsd_row[:, :], ws_down).then_inc(wsd_in, 16)
            sp.dma_start(gu_raw[1].rearrange("p (k n) -> p k n", k=KT),
                         w_gate.rearrange("(k p) n -> p k n", p=P)).then_inc(gu_in[1], 16)
            sp.wait_ge(c_lo_split, 1)
            sp.dma_start(raw[:, :].rearrange("p (k n) -> p k n", k=IT),
                         w_down.rearrange("(k p) n -> p k n", p=P)).then_inc(down_in, 16)
            sp.wait_ge(w_lo_split, 1)
            sp.dma_start(drive[:, 0:T * SW], x_state).then_inc(drive_in, 16)

            def chunk_io(h, first):
                if not first:
                    sp.wait_ge(out_done, 16 * h)
                sp.dma_start(x_res[:, :, :],
                             x_rows[bass.ds(h * RT * P, RT * P), :].rearrange("(a p) n -> p a n", p=P)
                             ).then_inc(x_in, 16)
                sp.wait_ge(y_ready, RT * h + RT)
                sp.dma_start(out[bass.ds(h * RT * P, RT * P), :].rearrange("(a p) n -> p a n", p=P),
                             y_sb[:, :, :]).then_inc(out_done, 16)

            chunk_io(0, True)
            with sp.Fori(1, CHUNKS) as h:
                chunk_io(h, False)
            sp.wait_ge(out_done, 16 * CHUNKS)

        @block.scalar
        def _(act):
            act.wait_ge(ones_set, 2)
            act.activation(warm[:, :], warm[:, :], ACT.Silu).then_inc(table_warm, 1)
            for i, hi in enumerate((wu_hi, wg_hi)):
                act.wait_ge(scale_set, i + 1)
                act.activation(hi[:, :], gu_raw[i], ACT.Identity,
                               scale=wscale[:, i:i + 1]).then_inc(w_hi_split, 1)
            act.wait_ge(wsd_spread, 1)
            act.activation(wsd_all[:, :], ps_had[:, :], ACT.Copy).then_inc(wsd_set, 1)
            act.wait_ge(drive_in, 16)
            act.wait_ge(bias_set, 1)
            drive_v = drive[:, 0:T * SW].rearrange("p (t k b) -> p t k b", k=KT, b=B)
            for kt in range(KT):
                act.activation(drive_v[:, :, kt, :], drive_v[:, :, kt, :], ACT.Identity, scale=S,
                               bias=bias[:, kt:kt + 1]).then_inc(drive_set, 1)
            act.wait_ge(d_scale_set, 1)

            def q_high(now, at):
                act.wait_ge(rclip_ready, now)
                act.activation(q_parts[:, bass.ds(at, SW)], r_clip[:, :], ACT.Copy,
                               scale=AQ[0] / S).then_inc(qhi_ready, 1)

            def stage(s, now, at):
                i = s % 4
                for x in range(2):
                    act.wait_ge(r_ready[i][x], now)
                    act.activation(t_parts[:, 2 * x:2 * x + 2, 0, :],
                                   half(r[:, i, :], x).rearrange("p (k b) -> p k b", b=B),
                                   ACT.Tanh, scale=AQ[i] / S).then_inc(thi_ready[i][x], 1)
                for x in range(2):
                    act.activation(half(t_full[:, :], x), half(r[:, i, :], x), ACT.Tanh,
                                   scale=AQ[i] / S).then_inc(tfull_ready[i][x], 1)
                c = A[i] * EPSILON
                src = r[:, i, :]
                if i == 0:
                    act.wait_ge(rclip_ready, now)
                    src = r_clip[:, :]
                if i < 3:
                    act.activation(p_drive[:, i, :], src, ACT.Copy,
                                   scale=c * AQ[i]).then_inc(pdrive_ready[i], 1)
                    if i:
                        act.wait_ge(pnext_ready[i], now)
                    else:
                        act.wait_ge(p_ready, now)
                    act.activation(p_decay[:, i, :], p[:, i, :], ACT.Copy,
                                   scale=c * BETA).then_inc(pdecay_ready[i], 1)
                act.activation(p_part[:, i, :], src, ACT.Copy,
                               scale=P_FROM[i] * AQ[i]).then_inc(ppart_ready[i], 1)
                if i == 0:
                    act.activation(p_part[:, 4, :], p[:, 0, :], ACT.Copy,
                                   scale=P_SELF).then_inc(pself_ready, 1)
                if i == 1:
                    act.wait_ge(push_ready[0], now)
                    q_high(now, at)

            def ffn(c, j, n, s, had, gate, down):
                if down and s == 3:
                    act.wait_ge(hid_ready, n - 17)
                    act.wait_ge(down_done, n - 18)
                    act.activation(hid_hi[:, :], hid[:, :], ACT.Copy).then_inc(hidhi_ready, 1)
                if gate and s == 7:
                    act.wait_ge(gate_done, n - 16)
                    act.wait_ge(hid_ready, n - 17)
                    act.activation(sil[:, :], ps_gate[:, 0:ROWS], ACT.Silu,
                                   scale=gscale[:, bass.ds((n - 17) % IT, 1)]).then_inc(sil_ready, 1)
                if isinstance(c, int) and c == 0 and s == 3:
                    tile = bass.ds(n * N, N)
                    act.activation(wd_hi[:, tile], raw[:, tile], ACT.Identity,
                                   scale=dscale[:, bass.ds(n, 1)]).then_inc(wd_hi_split, 1)
                if had and s in (2, 3):
                    x = s - 2
                    act.wait_ge(had_done, 2 * (c - 1) + x + 1)
                    act.activation(xh_hi_f[:, bass.ds((c - 1) % 2 * (KT * ROWS) + x * 2 * ROWS,
                                                      2 * ROWS)],
                                   ps_rot[x][:, :], ACT.Copy).then_inc(xhi_ready, 1)

            def body(c, j, n, recur, had, gate, down, follows):
                if recur:
                    now = step_counts(act, n)
                    at = [c_ * 2 * SW for c_ in now]
                for s_ in range(SLOTS):
                    if recur:
                        stage(s_, now[s_ // 4], at[s_ // 4])
                    ffn(c, j, n, s_, had, gate, down)

            run_bodies(act, body, lambda: q_high(T + 1, (T + 1) * 2 * SW))

        @block.tensor
        def _(pe):
            pe.wait_ge(ident_in, 16)
            pe.wait_ge(ones_set, 1)
            for i in range(2):
                pe.wait_ge(peaks_found, i + 1)
                pe.transpose(ps_had[0:1, 0:P], peak[:, i:i + 1], ident[:, :]).then_inc(peaks_turned, 1)
                pe.wait_ge(top_found, i + 1)
                pe.matmul(ps_had[:, 0:1], ones[:, :], top[:, 2 * i + 1:2 * i + 2],
                          start=True, stop=True).then_inc(top_spread, 1)
            pe.wait_ge(wsd_in, 16)
            pe.wait_ge(unscale_set, 2)
            pe.matmul(ps_had[:, :], ones[:, :], wsd_row[:, :], start=True, stop=True).then_inc(wsd_spread, 1)
            pe.wait_ge(had_in, 16)
            pe.wait_ge(fly_add, 8)
            pe.wait_ge(fly_sub, 4)
            for i in range(IT):
                if i >= 2:
                    pe.wait_ge(wd_scaled, i - 1)
                pe.matmul([ps_gate, ps_up][i % 2][:, :], h128[:, :], raw[:, i * N:(i + 1) * N],
                          start=True, stop=True).then_inc(wd_rotated, 1)
            pe.wait_ge(wsd_set, 1)
            pe.wait_ge(had_set, 1)
            pe.wait_ge(c_lo_split, 1)

            def couple(w, x, m, moving, first=False, last=False):
                for a in m:
                    o = (a % 2) * B
                    for kt in (2 * x, 2 * x + 1):
                        done = pe.matmul(
                            prod[a // 2][:, 0:moving, o:o + B], w[:, kt, a * P:(a + 1) * P],
                            t_parts[:, kt, 0:moving, :], start=(first and a % 2 == 0 and kt == 0),
                            stop=(last and a % 2 == 1 and kt == KT - 1), skip_group_check=True)
                return done

            def stage(s, now):
                i = s % 4
                pe.wait_ge(thi_ready[i][0], now)
                couple(c_lo, 0, (0, 1), 1, first=True)
                pe.wait_ge(thi_ready[i][1], now)
                couple(c_lo, 0, (2, 3), 1, first=True)
                couple(c_lo, 1, (0, 1, 2, 3), 1)
                pe.wait_ge(tlo_ready[i][0], now)
                couple(c_hi, 0, (0, 1, 2, 3), 2)
                pe.wait_ge(tlo_ready[i][1], now)
                for h in range(2):
                    couple(c_hi, 1, (2 * h, 2 * h + 1), 2, last=True).then_inc(prod_ready[i][h], 1)

            def keep_clock(unused):
                n = unused.shape[-1] // P
                pe.matmul(unused, had_p[:, 0, :], had_p[:, 0:n, :].rearrange("p k n -> p (k n)"),
                          start=True, stop=True, skip_group_check=True)

            def rotate(c, n, x, recur, had_at):
                if x == 0:
                    pe.wait_ge(qlo_ready, c * CHUNK_STEPS + 1)
                    pe.wait_ge(wsd_set, 1)
                    if not (isinstance(c, int) and c == 1):
                        pe.wait_ge(xlo_ready, 2 * (c - 1))
                elif not recur:
                    pe.wait_ge(hid_ready, n - 17)
                base = q_parts[:, bass.ds(had_at, CHUNK_STEPS * 2 * SW)].rearrange(
                    "p (t a k b) -> p t a k b", a=2, k=KT, b=B)
                for o in range(2):
                    for kt in range(KT):
                        sign = bin((2 * x + o) & kt).count("1") % 2
                        for part in range(2):
                            last = pe.matmul(ps_rot[x][:, o * ROWS:(o + 1) * ROWS].rearrange(
                                                 "p (t b) -> p t b", b=B),
                                             (had_m if sign else had_p)[:, kt, :],
                                             base[:, :, part, kt, :],
                                             start=(kt == 0 and part == 0 and o == 0),
                                             stop=(kt == 3 and part == 1 and o == 1),
                                             skip_group_check=True)
                last.then_inc(had_done, 1)

            def ffn(c, j, n, s, recur, now, had, gate, down, tile, rows_at, down_tile, had_at):
                if had and s == 2:
                    rotate(c, n, 0, recur, had_at)
                    rotate(c, n, 1, recur, had_at)
                if gate:
                    share = GU_SHARE_HAD if had else GU_SHARE
                    for m in range(sum(share[:s]), sum(share[:s + 1])):
                        side, kt, x = m // 12, m // 3 % 4, m % 3
                        a, b = ((0, 0), (1, 0), (0, 1))[x]
                        w = ((wg_hi, wg_lo), (wu_hi, wu_lo))[side][a]
                        bank, ready = ((ps_gate, gate_done), (ps_up, up_done))[side]
                        xs = (xh_hi_f, xh_lo_f)[b]
                        if m == 0 and not recur:
                            pe.wait_ge(sil_ready, n - 17)
                        if m == 12 and not recur:
                            pe.wait_ge(hid_ready, n - 17)
                        if m == 12 and had:
                            pe.wait_ge(xlo_ready, 2 * (c - 1) + 2)
                        if isinstance(j, int) and j == 1 and m in (0, 6):
                            pe.wait_ge(xhi_ready, 2 * (c - 1) + 1 + m // 6)
                            pe.wait_ge(xlo_ready, 2 * (c - 1) + 1 + m // 6)
                        last = pe.matmul(bank[:, 0:ROWS],
                                         w[:, kt * INTER:(kt + 1) * INTER][:, bass.ds(tile, P)],
                                         xs[:, bass.ds(rows_at + kt * ROWS, ROWS)],
                                         start=(kt == 0 and x == 0), stop=(kt == 3 and x == 2))
                        if m % 12 == 11:
                            last.then_inc(ready, 1)
                for m in range(6):
                    if not down or DOWN_SLOTS[m] != s:
                        continue
                    a, x = m // 3, m % 3
                    if x == 0:
                        pe.wait_ge(hidlo_ready, 2 * (n - 18) + a + 1)
                    first = isinstance(j, int) and j == 2
                    if first and m == 0 and isinstance(c, int) and c == 1:
                        pe.wait_ge(wd_lo_split, 2 * IT)
                    end = isinstance(j, int) and j == 1
                    if first and x == 0 and not (isinstance(c, int) and c == 1):
                        pe.wait_ge(y_ready, RT * (c - 2) + a + 1)
                    last = pe.matmul(ps_y[a][:, :], (hid_hi, hid_hi, hid_lo)[x][:, a * P:(a + 1) * P],
                                     (wd_hi, wd_lo, wd_hi)[x][:, bass.ds(down_tile, N)],
                                     start=(first and x == 0), stop=(end and x == 2),
                                     skip_group_check=True)
                    if m == 5:
                        last.then_inc(down_done, 1)

            def body(c, j, n, recur, had, gate, down, follows):
                fixed = isinstance(n, int)
                hold = (lambda v: v) if fixed else pe.snap
                now = step_counts(pe, n) if recur else None
                tile = hold((n - 17) % IT * P) if gate else None
                rows_at = hold((n - 17) // BODIES % 2 * (KT * ROWS)) if gate else None
                down_tile = hold((n - 18) % IT * N) if down else None
                had_at = ((c - 1) * CHUNK_STEPS + 2) * 2 * SW if had else None
                if had and not isinstance(c, int):
                    had_at = pe.snap(had_at)
                for s_ in range(SLOTS):
                    if recur:
                        stage(s_, now[s_ // 4])
                    ffn(c, j, n, s_, recur, now[s_ // 4] if recur else None, had, gate, down, tile, rows_at, down_tile, had_at)
                    if recur and gate:
                        for _ in range((FILL_HAD if had else FILL)[s_]):
                            keep_clock(ps_had[:, 0:2 * P])

            run_bodies(pe, body)

        @block.vector
        def _(dve):
            dve.memset(ones[:, :], 1.0).then_inc(ones_set, 1)
            dve.memset(warm[:, :], 0.0).then_inc(ones_set, 1)
            dve.wait_ge(c_in, 16)
            c_hi_f, c_lo_f = [c[:, :, :].rearrange("p k n -> p (k n)") for c in (c_hi, c_lo)]
            dve.tensor_scalar(c_hi_f, c_raw, S, None, ALU.mult).then_inc(c_hi_split, 1)
            dve.wait_ge(c_hi_split, 1)
            dve.scalar_tensor_tensor(out=c_lo_f, in0=c_raw, scalar=S, in1=c_hi_f, op0=ALU.mult,
                                     op1=ALU.subtract).then_inc(c_lo_split, 1)
            dve.wait_ge(had_in, 16)
            for kt in range(KT):
                sign = vec[:, V_SUUG + kt:V_SUUG + kt + 1]
                dve.tensor_scalar(had_p[:, kt, :], h128[:, :], sign, None, ALU.mult)
                last = dve.tensor_scalar(had_m[:, kt, :], h128[:, :], sign, -1.0, ALU.mult, ALU.mult)
            last.then_inc(had_set, 1)
            for i in range(2):
                dve.wait_ge(gu_in[i], 16)
                dve.tensor_reduce(peak[:, i:i + 1], gu_raw[i], AX.X, ALU.max,
                                  apply_absolute_value=True).then_inc(peaks_found, 1)
                dve.wait_ge(peaks_turned, i + 1)
                dve.tensor_reduce(top[:, 2 * i:2 * i + 1], ps_had[0:1, 0:P], AX.X,
                                  ALU.max).then_inc(scales_step, 1)
                dve.wait_ge(scales_step, i + 1)
                dve.tensor_scalar(top[:, 2 * i + 1:2 * i + 2], top[:, 2 * i:2 * i + 1],
                                  1.0 / FP16_TOP, 1e-30, ALU.mult, ALU.max).then_inc(top_found, 1)
                dve.wait_ge(top_spread, i + 1)
                dve.tensor_copy(unscale[:, i:i + 1], ps_had[:, 0:1]).then_inc(unscale_set, 1)
                dve.wait_ge(unscale_set, i + 1)
                dve.reciprocal(wscale[:, i:i + 1], unscale[:, i:i + 1]).then_inc(scale_set, 1)
            dve.wait_ge(scale_set, 2)
            for i, (hi, lo) in enumerate(((wu_hi, wu_lo), (wg_hi, wg_lo))):
                dve.wait_ge(w_hi_split, i + 1)
                dve.scalar_tensor_tensor(out=lo[:, :], in0=gu_raw[i], scalar=wscale[:, i:i + 1],
                                         in1=hi[:, :], op0=ALU.mult,
                                         op1=ALU.subtract).then_inc(w_lo_split, 1)
            dve.wait_ge(vec_in, 16)
            dve.tensor_scalar(bias[:, :], vec[:, V_BIAS:V_BIAS + KT], P_SHIFT, S, ALU.subtract,
                              ALU.mult).then_inc(bias_set, 1)
            dve.wait_ge(down_in, 16)
            dve.wait_ge(w_lo_split, 2)
            for lv in range(4):
                sum_out, diff_out, a, b = butterfly(lv)
                if lv:
                    dve.wait_ge(fly_add, 2 * lv)
                    dve.wait_ge(fly_sub, lv)
                w = a.shape[-1] // 3
                dve.tensor_tensor(sum_out, a, b, ALU.add).then_inc(fly_add, 1)
                dve.tensor_tensor(diff_out[:, :, 0:w], a[:, :, 0:w], b[:, :, 0:w],
                                  ALU.subtract).then_inc(fly_add, 1)
            dve.wait_ge(wsd_set, 1)
            for i in range(IT):
                dve.wait_ge(wd_rotated, i + 1)
                dve.tensor_tensor(raw[:, i * N:(i + 1) * N], [ps_gate, ps_up][i % 2][:, :],
                                  wsd_all[:, :], ALU.mult).then_inc(wd_scaled, 1)
            dve.wait_ge(wd_scaled, IT)
            dve.tensor_reduce(dpeak[:, :], raw[:, :].rearrange("p (i n) -> p i n", n=N), AX.X,
                              ALU.max, apply_absolute_value=True).then_inc(scales_step, 1)
            dve.wait_ge(scales_step, 3)
            dve.tensor_scalar(dunscale[:, :], dpeak[:, :], 1.0 / FP16_TOP, 1e-30, ALU.mult,
                              ALU.max).then_inc(d_unscale_set, 1)
            dve.wait_ge(d_unscale_set, 1)
            dve.reciprocal(dscale[:, :], dunscale[:, :]).then_inc(d_scale_set, 1)
            root = float(N) ** -0.5
            dve.tensor_scalar(gscale[:, :], vec[:, V_WGATE:V_WGATE + IT], unscale[:, 1:2], root,
                              ALU.mult, ALU.mult)
            dve.tensor_scalar(utmp[:, 0, :], vec[:, V_WUP:V_WUP + IT], unscale[:, 0:1],
                              root * float(INTER) ** -0.5, ALU.mult, ALU.mult).then_inc(scales_step, 1)
            dve.wait_ge(scales_step, 4)
            dve.tensor_tensor(utmp[:, 1, :], utmp[:, 0, :], vec[:, V_SUDP:V_SUDP + IT],
                              ALU.mult).then_inc(scales_step, 1)
            dve.wait_ge(scales_step, 5)
            dve.tensor_tensor(uscale[:, :], utmp[:, 1, :], dunscale[:, :],
                              ALU.mult).then_inc(scales_step, 1)
            dve.wait_ge(cond_in, 16)
            dve.wait_ge(scales_step, 6)
            for x in range(2):
                dve.tensor_scalar(half(r[:, 0, :], x), half(q_cond[:, :], x), S / AQ[0], None,
                                  ALU.mult).then_inc(r_ready[0][x], 1)

            def t_low(i, x, now):
                dve.wait_ge(tfull_ready[i][x], now)
                dve.tensor_tensor(t_parts[:, 2 * x:2 * x + 2, 1, :],
                                  half(t_full[:, :], x).rearrange("p (k b) -> p k b", b=B),
                                  t_parts[:, 2 * x:2 * x + 2, 0, :],
                                  ALU.subtract).then_inc(tlo_ready[i][x], 1)

            def clip(now, first):
                bound = CLAMP * S / AQ[0]
                dve.wait_ge(r_ready[0][1], now)
                if first:
                    step = dve.tensor_scalar(r_clip[:, :], r[:, 0, :], 1.0, None, ALU.mult)
                else:
                    step = dve.tensor_scalar(r_clip[:, :], r[:, 0, :], bound, -bound, ALU.min,
                                             ALU.max)
                step.then_inc(rclip_ready, 1)

            def q_low(now, at):
                dve.wait_ge(qhi_ready, now)
                dve.scalar_tensor_tensor(out=q_parts[:, bass.ds(at + SW, SW)], in0=r_clip[:, :],
                                         scalar=AQ[0] / S, in1=q_parts[:, bass.ds(at, SW)],
                                         op0=ALU.mult, op1=ALU.subtract).then_inc(qlo_ready, 1)

            def stage(s, now, at, first):
                i = s % 4
                src = r_clip[:, :] if i == 0 else r[:, i, :]

                def square():
                    if i:
                        dve.wait_ge(r_ready[i][1], now)
                    else:
                        dve.wait_ge(rclip_ready, now)
                    dve.scalar_tensor_tensor(out=q_sq[:, i, :], in0=src,
                                             scalar=-(AQ[i] / S) ** 2 / 3, in1=src, op0=ALU.mult,
                                             op1=ALU.mult).then_inc(sq_ready[i], 1)

                def cubic():
                    dve.wait_ge(sq_ready[i], now)
                    dve.scalar_tensor_tensor(out=fq[:, i, :], in0=q_sq[:, i, :], scalar=1.0,
                                             in1=src, op0=ALU.add, op1=ALU.mult).then_inc(fq_ready[i], 1)

                def rest():
                    if i < 3:
                        dve.wait_ge(push_ready[i], now)
                        in0, scale, in1 = r_clip[:, :], BASE[i], push[:, i, :]
                    else:
                        dve.wait_ge(accpush_ready, now)
                        in0, scale, in1 = r[:, 3, :], 2.0, acc_push[:, :]
                    dve.scalar_tensor_tensor(out=base_push[:, i, :], in0=in0, scalar=scale, in1=in1,
                                             op0=ALU.mult, op1=ALU.add).then_inc(bpush_ready[i], 1)

                if i == 2:
                    dve.scalar_tensor_tensor(out=r_acc[:, 0, :], in0=r_clip[:, :],
                                             scalar=-BASE_EXCESS, in1=r[:, 1, :], op0=ALU.mult,
                                             op1=ALU.add).then_inc(acc1_ready, 1)
                if i == 3:
                    dve.wait_ge(acc1_ready, now)
                    dve.scalar_tensor_tensor(out=r_acc[:, 1, :], in0=r[:, 2, :], scalar=2.0,
                                             in1=r_acc[:, 0, :], op0=ALU.mult,
                                             op1=ALU.add).then_inc(acc2_ready, 1)
                if i == 0:
                    clip(now, first)
                    square()
                    t_low(i, 0, now)
                    cubic()
                    t_low(i, 1, now)
                    rest()
                elif i < 3:
                    square()
                    rest()
                    cubic()
                    t_low(i, 0, now)
                    t_low(i, 1, now)
                else:
                    square()
                    cubic()
                    t_low(i, 0, now)
                    t_low(i, 1, now)
                    rest()
                dve.wait_ge(bpush_ready[i], now)
                dve.wait_ge(fq_ready[i], now)
                dve.scalar_tensor_tensor(out=b_full, in0=halves(fq[:, i, :]), scalar=AQ[i],
                                         in1=halves(base_push[:, i, :]), op0=ALU.mult,
                                         op1=ALU.add).then_inc(bfull_ready[i], 1)
                if i == 2:
                    q_low(now, at)

            def next_r(s, now):
                i = s % 4
                for x in range(2):
                    dve.wait_ge(prod_ready[i][x], now)
                    if x == 0:
                        dve.wait_ge(bfull_ready[i], now)
                    dve.tensor_reduce(half(r[:, (i + 1) % 4, :], x), sum_full[x], AX.X,
                                      ALU.add).then_inc(r_ready[(i + 1) % 4][x], 1)

            def down_low(n, x):
                cols = bass.ds(n * N + x * (N // 2), N // 2)
                dve.scalar_tensor_tensor(out=wd_lo[:, cols], in0=raw[:, cols],
                                         scalar=dscale[:, bass.ds(n, 1)], in1=wd_hi[:, cols],
                                         op0=ALU.mult, op1=ALU.subtract).then_inc(wd_lo_split, 1)

            def rotated_low(c, x, at):
                place = bass.ds(at + x * 2 * ROWS, 2 * ROWS)
                dve.wait_ge(xhi_ready, 2 * (c - 1) + x + 1)
                dve.tensor_tensor(xh_lo_f[:, place], ps_rot[x][:, :], xh_hi_f[:, place],
                                  ALU.subtract).then_inc(xlo_ready, 1)

            def hidden(n, recur):
                if not recur:
                    dve.wait_ge(hidlo_ready, 2 * (n - 18))
                    dve.wait_ge(sil_ready, n - 17)
                    dve.wait_ge(up_done, n - 17)
                dve.scalar_tensor_tensor(out=hid[:, :], in0=ps_up[:, 0:ROWS],
                                         scalar=uscale[:, bass.ds((n - 18) % IT, 1)], in1=sil[:, :],
                                         op0=ALU.mult, op1=ALU.mult).then_inc(hid_ready, 1)

            def output(c, a):
                dve.wait_ge(down_done, (c - 1) * BODIES)
                dve.wait_ge(x_in, 16 * (c - 1))
                dve.tensor_tensor(y_sb[:, a, :], ps_y[a][:, :], x_res[:, a, :],
                                  ALU.add).then_inc(y_ready, 1)

            next_step = []

            def body(c, j, n, recur, had, gate, down, follows):
                hold = (lambda v: v) if isinstance(n, int) else dve.snap
                first = isinstance(n, int) and n == 0
                if recur:
                    now = next_step.pop() if follows else hold(n * BODY_STEPS + 1)
                    next_step.clear()
                for s_ in range(SLOTS):
                    if recur:
                        if s_ == 4:
                            now = after
                        stage(s_, now, at if s_ % 4 == 2 else None, first and s_ == 0)
                    if had and s_ == 2:
                        had_at = (c - 1) % 2 * (KT * ROWS)
                        if not isinstance(c, int):
                            had_at = dve.snap(had_at)
                    if recur and s_ % 4 == 1:
                        at = hold(now * (2 * SW))
                    if recur and s_ == 2:
                        after = hold(now + 1)
                    if recur and s_ == 6:
                        next_step.append(hold(now + 1))
                    if isinstance(c, int) and c == 0 and s_ in (5, 6):
                        down_low(n, s_ - 5)
                    if had and s_ == 3:
                        rotated_low(c, 1, had_at)
                    if down and s_ == 1:
                        hidden(n, recur)
                    if (isinstance(j, int) and j == 2 and s_ in (2, 5)
                            and not (isinstance(c, int) and c == 1)):
                        output(c, s_ // 3)
                    if recur:
                        next_r(s_, now)
                    if had and s_ == 2:
                        rotated_low(c, 0, had_at)

            def last_q():
                clip(T + 1, False)
                q_low(T + 1, (T + 1) * 2 * SW)

            run_bodies(dve, body, last_q, group=6, first_group=5)

        @block.gpsimd
        def _(pool):
            pool.wait_ge(cond_in, 16)
            pool.tensor_scalar(p[:, 0, :], q_cond[:, :], S, -S * P_SHIFT, ALU.mult,
                               ALU.add).then_inc(p_ready, 1)
            pool.wait_ge(down_in, 16)
            pool.wait_ge(w_lo_split, 2)
            for lv in range(4):
                _, diff_out, a, b = butterfly(lv)
                if lv:
                    pool.wait_ge(fly_add, 2 * lv)
                    pool.wait_ge(fly_sub, lv)
                w = a.shape[-1] // 3
                pool.tensor_tensor(diff_out[:, :, w:], a[:, :, w:], b[:, :, w:],
                                   ALU.subtract).then_inc(fly_sub, 1)
            pool.wait_ge(drive_set, KT)

            def wait_apart(signal, count):
                count = pool.snap(count) if not isinstance(count, int) else count
                pool.wait_ge(cond_in, 16)
                pool.wait_ge(signal, count)

            def stage(s, now, at):
                i = s % 4
                if i == 0:
                    pool.wait_ge(p_ready, now)
                    pool.tensor_tensor(push[:, 0, :], track[:, bass.ds(at, SW)], p[:, 0, :],
                                       ALU.subtract).then_inc(push_ready[0], 1)
                if i < 3:
                    pool.wait_ge(pdrive_ready[i], now)
                    pool.wait_ge(pdecay_ready[i], now)
                    pool.tensor_tensor(p_move[:, i, :], p_drive[:, i, :], p_decay[:, i, :],
                                       ALU.subtract).then_inc(pmove_ready[i], 1)
                    pool.wait_ge(pmove_ready[i], now)
                    pool.tensor_tensor(push[:, i + 1, :], push[:, 0, :], p_move[:, i, :],
                                       ALU.subtract).then_inc(push_ready[i + 1], 1)
                if i < 2:
                    pool.tensor_tensor(p[:, i + 1, :], p[:, 0, :], p_move[:, i, :],
                                       ALU.add).then_inc(pnext_ready[i + 1], 1)
                if i < 3:
                    pool.wait_ge(ppart_ready[i], now)
                    if i == 0:
                        pool.wait_ge(pself_ready, now)
                    else:
                        pool.wait_ge(pacc_ready[i - 1], now)
                    pool.tensor_tensor(p_acc[:, i, :], p_part[:, 4, :] if i == 0 else p_acc[:, i - 1, :],
                                       p_part[:, i, :], ALU.add).then_inc(pacc_ready[i], 1)
                if i == 3:
                    pool.wait_ge(push_ready[3], now)
                    pool.wait_ge(acc2_ready, now)
                    pool.tensor_tensor(acc_push[:, :], r_acc[:, 1, :], push[:, 3, :],
                                       ALU.add).then_inc(accpush_ready, 1)
                if i == 3:
                    pool.wait_ge(pacc_ready[2], now)
                    pool.tensor_tensor(p_acc[:, 3, :], p[:, 0, :], p_acc[:, 2, :],
                                       ALU.add).then_inc(pacc_ready[3], 1)
                    pool.wait_ge(ppart_ready[3], now)
                    pool.wait_ge(pacc_ready[3], now)
                    pool.tensor_tensor(p_raw[:, :], p_acc[:, 3, :], p_part[:, 3, :],
                                       ALU.add).then_inc(praw_ready, 1)
                    wait_apart(praw_ready, now)
                    pool.tensor_scalar(p[:, 0, :], p_raw[:, :], (CLAMP - P_SHIFT) * S,
                                       (-CLAMP - P_SHIFT) * S, ALU.min, ALU.max).then_inc(p_ready, 1)

            def ffn(c, j, n, s, had, gate, down):
                if down and s in (5, 6):
                    a = s - 5
                    rows = slice(a * P, (a + 1) * P)
                    pool.wait_ge(hidhi_ready, n - 17)
                    pool.tensor_tensor(hid_lo[:, rows], hid[:, rows], hid_hi[:, rows],
                                       ALU.subtract).then_inc(hidlo_ready, 1)

            def body(c, j, n, recur, had, gate, down, follows):
                if recur:
                    now = step_counts(pool, n)
                    at = [c_ * SW for c_ in now]
                for s_ in range(SLOTS):
                    ffn(c, j, n, s_, had, gate, down)
                    if recur:
                        stage(s_, now[s_ // 4], at[s_ // 4])

            run_bodies(pool, body)

def _hadamard():
    h = np.ones((1, 1), np.float32)
    while h.shape[0] < P:
        h = np.block([[h, h], [h, -h]])
    return np.ascontiguousarray(h.astype(np.float32))


def kernel(x, cond_2048, L0_cond_coupling, L0_cond_bias, L0_ffn_SU_ug, L0_ffn_SU_dp,
           L0_ffn_Wscale_ug, L0_ffn_Wscale_dp, L0_ffn_W_up, L0_ffn_W_gate, L0_ffn_W_down):
    import concourse.bacc as bacc
    from concourse.bass_utils import run_bass_kernel_spmd

    def columns(v):
        return np.asarray(v).reshape(-1, P).T

    x = np.asarray(x)
    arrays = {
        "x_state": x.reshape(B, T, KT, P).transpose(3, 1, 2, 0).reshape(P, T * SW),
        "x_rows": x.transpose(1, 0, 2).reshape(T * B, N),
        "cond": np.asarray(cond_2048).reshape(B, KT, P).transpose(2, 1, 0).reshape(P, SW),
        "coupling": np.asarray(L0_cond_coupling).T,
        "w_up": np.asarray(L0_ffn_W_up).T,
        "w_gate": np.asarray(L0_ffn_W_gate).T,
        "w_down": np.asarray(L0_ffn_W_down).T,
        "vectors": np.concatenate([columns(L0_cond_bias), columns(L0_ffn_SU_ug),
                                   columns(L0_ffn_Wscale_ug), columns(L0_ffn_SU_dp)], axis=1),
        "ws_down": np.asarray(L0_ffn_Wscale_dp).reshape(1, N),
        "hadamard": _hadamard(),
        "identity": np.eye(P, dtype=np.float32),
    }
    arrays = {n: np.ascontiguousarray(a) for n, a in arrays.items()}
    nc = bacc.Bacc("TRN2", target_bir_lowering=False, num_devices=1)
    args = {n: nc.dram_tensor("in_" + n, a.shape, mybir.dt.from_np(a.dtype), kind="ExternalInput").ap()
            for n, a in arrays.items()}
    out = nc.dram_tensor("out_rows", (T * B, N), F32, kind="ExternalOutput").ap()
    build(nc, out=out, **args)
    res = run_bass_kernel_spmd(nc, [{"in_" + n: a for n, a in arrays.items()}], core_ids=[0])
    rows = res.results[0]["out_rows"]
    return np.ascontiguousarray(rows.reshape(T, B, N).transpose(1, 0, 2))
```
